# Optimizing a Trainium2 kernel written in Bass

```python
import numpy as np
import jax
import jax.numpy as jnp

def _softmax(x, axis=-1):
    return jax.nn.softmax(x, axis=axis)

def _gelu(x):
    return jax.nn.gelu(x, approximate=True)

def _silu(x):
    return jax.nn.silu(x)

def _sigmoid(x):
    return jax.nn.sigmoid(x)

def _layernorm(x, axis=-1, eps=1e-05):
    m = jnp.mean(x, axis=axis, keepdims=True)
    v = jnp.var(x, axis=axis, keepdims=True)
    return (x - m) / jnp.sqrt(v + eps)

def _scatter_add(tgt, idx, src, axis=0):
    return tgt.at[idx].add(src)

def _segment_sum(src, seg, n):
    return jax.ops.segment_sum(src, seg, n)
kernel_name = 'mk_gnn_preln_d4_gnn_r16_407f0b'

def setup_inputs(seed: int=0):
    np.random.seed(seed)
    _w = jnp.asarray

    def _rec_inputs():
        import jax
        import jax.numpy as jnp
        _gk = jax.random.key(seed)
        x = -0.0005121 + 1.001 * jax.random.normal(jax.random.fold_in(_gk, 1), (6250, 32), jnp.float32)
        _s = jax.random.randint(jax.random.fold_in(_gk, 2), (100000,), 0, 6250, jnp.int32)
        _d = jax.random.randint(jax.random.fold_in(_gk, 3), (100000,), 0, 6250, jnp.int32)
        _loop = jnp.arange(6250, dtype=jnp.int32)
        src = jnp.concatenate([_s, _d, _loop])
        dst = jnp.concatenate([_d, _s, _loop])
        _o = jnp.argsort(dst, stable=True)
        src = src[_o]
        dst = dst[_o]
        edge_attr_3 = jax.random.uniform(jax.random.fold_in(_gk, 12), (206250, 3), jnp.float32, 0.0, 1)
        edge_type_4 = jax.random.randint(jax.random.fold_in(_gk, 14), (206250,), 0, 4, jnp.int32)
        edge_weight = jax.random.uniform(jax.random.fold_in(_gk, 15), (206250,), jnp.float32, 0.0, 1)
        return (x, src, dst, edge_attr_3, edge_type_4, edge_weight)
    x, src, dst, edge_attr_3, edge_type_4, edge_weight = _rec_inputs()

    def _L0_gnn_setup():
        import jax, jax.numpy as jnp
        import numpy as np
        N_NODES = 6250
        N_EDGES = 100000
        LATENT_DIM = 32
        NUM_LAYERS = 3
        key = jax.random.key(seed)
        k_x, k_e = jax.random.split(key)
        x = jax.random.normal(k_x, (N_NODES, LATENT_DIM), dtype=jnp.float32)
        edge_index = jax.random.randint(k_e, (2, N_EDGES), 0, N_NODES, dtype=jnp.int64)
        return {'x': x, 'edge_index': edge_index, 'num_layers': NUM_LAYERS}
    _L0_gnn_all = _L0_gnn_setup()
    _L0_gnn_in = {k: v for k, v in _L0_gnn_all.items() if k in ()}
    del _L0_gnn_all

    def _L1_gnn_setup():
        import jax, jax.numpy as jnp
        import numpy as np
        N_NODES = 6250
        N_EDGES = 100000
        EMB_DIM = 32
        NUM_LAYERS = 3
        key = jax.random.key(seed)
        k_emb, k_w, k_row, k_col = jax.random.split(key, 4)
        emb = jax.random.normal(k_emb, (N_NODES, EMB_DIM), dtype=jnp.float32)
        edge_weight = jax.random.uniform(k_w, (N_EDGES,), dtype=jnp.float32)
        row = jax.random.randint(k_row, (N_EDGES,), 0, N_NODES, dtype=jnp.int32)
        col = jax.random.randint(k_col, (N_EDGES,), 0, N_NODES, dtype=jnp.int32)
        return {'emb': emb, 'edge_weight': edge_weight, 'row': row, 'col': col, 'num_layers': NUM_LAYERS}
    _L1_gnn_all = _L1_gnn_setup()
    _L1_gnn_in = {k: v for k, v in _L1_gnn_all.items() if k in ()}
    del _L1_gnn_all

    def _L2_gnn_setup():
        import jax, jax.numpy as jnp
        import numpy as np
        N = 3125
        E = 100000
        C = 32
        KS = 4
        DIM = 3
        K3 = KS ** DIM
        NEG = 0.01
        EPS = 1e-05
        _BITS = np.array([[s >> d & 1 for d in range(DIM)] for s in range(2 ** DIM)], dtype=np.int32)

        def _basis(edge_attr):
            v = edge_attr * (KS - 1)
            lo = jnp.floor(v)
            f = v - lo
            lo = lo.astype(jnp.int32)
            bits = jnp.asarray(_BITS)
            idx = jnp.clip(lo[:, None, :] + bits[None], 0, KS - 1)
            w = jnp.where(bits[None] == 1, f[:, None, :], 1.0 - f[:, None, :])
            basis = jnp.prod(w, axis=-1)
            wi = idx[..., 0] + KS * idx[..., 1] + KS * KS * idx[..., 2]
            return (basis, wi)

        def _sconv(x, src, dst, basis, wi, W, R, b):
            n = x.shape[0]
            z = jnp.einsum('nc,kco->nko', x, W)
            msg = jnp.zeros((src.shape[0], W.shape[2]), x.dtype)
            for s in range(basis.shape[1]):
                msg = msg + basis[:, s, None] * z[src, wi[:, s]]
            agg = jax.ops.segment_sum(msg, dst, num_segments=n)
            cnt = jax.ops.segment_sum(jnp.ones((dst.shape[0],), x.dtype), dst, num_segments=n)
            agg = agg / jnp.clip(cnt, 1.0)[:, None]
            return agg + x @ R + b

        def _bn(x, g, be):
            mu = x.mean(0)
            var = x.var(0)
            return (x - mu) * jax.lax.rsqrt(var + EPS) * g + be

        def _leaky(x):
            return jnp.where(x >= 0, x, NEG * x)
        key = jax.random.key(seed)
        ks = jax.random.split(key, 32)
        inp = {'patch_embs': jax.random.normal(ks[0], (N, C), jnp.float32), 'edge_index': jax.random.randint(ks[1], (2, E), 0, N, jnp.int32), 'edge_attr': jax.random.uniform(ks[2], (E, DIM), jnp.float32)}
        i = 3
        for l in (1, 2, 3):
            inp[f'W{l}'] = jax.random.normal(ks[i], (K3, C, C), jnp.float32) * 0.05
            i += 1
            inp[f'R{l}'] = jax.random.normal(ks[i], (C, C), jnp.float32) * 0.1
            i += 1
            inp[f'b{l}'] = jnp.zeros((C,), jnp.float32)
            inp[f'g{l}'] = jnp.ones((C,), jnp.float32)
            inp[f'be{l}'] = jnp.zeros((C,), jnp.float32)
        return inp
    _L2_gnn_all = _L2_gnn_setup()
    _L2_gnn_in = {k: v for k, v in _L2_gnn_all.items() if k in ('W1', 'R1', 'b1', 'g1', 'be1', 'W2', 'R2', 'b2', 'g2', 'be2', 'W3', 'R3', 'b3', 'g3', 'be3')}
    del _L2_gnn_all

    def _L3_gnn_setup():
        import jax, jax.numpy as jnp
        import numpy as np
        N_NODES = 6250
        IN_DIM = 32
        ENC_HID = 64
        OUT_DIM = 32
        N_EDGES = 100000

        def _gcn_forward(node_features, W1, b1, W2, b2, Wg, bg, src, dst):
            h0 = jax.nn.relu(node_features @ W1 + b1)
            h0 = jax.nn.relu(h0 @ W2 + b2)
            n = node_features.shape[0]
            loop = jnp.arange(n, dtype=src.dtype)
            s = jnp.concatenate([src, loop])
            d = jnp.concatenate([dst, loop])
            ones = jnp.ones(s.shape[0], dtype=h0.dtype)
            deg_out = jax.ops.segment_sum(ones, s, num_segments=n)
            deg_in = jax.ops.segment_sum(ones, d, num_segments=n)
            norm_src = jax.lax.rsqrt(jnp.clip(deg_out, 1.0))
            norm_dst = jax.lax.rsqrt(jnp.clip(deg_in, 1.0))
            m = (h0 * norm_src[:, None])[s]
            agg = jax.ops.segment_sum(m, d, num_segments=n)
            h1 = agg * norm_dst[:, None] @ Wg + bg
            h1 = jax.nn.relu(h1)
            return h0 + h1
        key = jax.random.key(seed)
        ks = jax.random.split(key, 10)
        node_features = jax.random.normal(ks[0], (N_NODES, IN_DIM), dtype=jnp.float32)
        edge_src = jax.random.randint(ks[1], (N_EDGES,), 0, N_NODES, dtype=jnp.int32)
        edge_dst = jax.random.randint(ks[2], (N_EDGES,), 0, N_NODES, dtype=jnp.int32)
        edgetypes = jax.random.randint(ks[3], (N_EDGES,), 0, 4, dtype=jnp.int32)
        s1 = 1.0 / np.sqrt(IN_DIM)
        s2 = 1.0 / np.sqrt(ENC_HID)
        W1 = jax.random.uniform(ks[4], (IN_DIM, ENC_HID), jnp.float32, -s1, s1)
        b1 = jax.random.uniform(ks[5], (ENC_HID,), jnp.float32, -s1, s1)
        W2 = jax.random.uniform(ks[6], (ENC_HID, OUT_DIM), jnp.float32, -s2, s2)
        b2 = jax.random.uniform(ks[7], (OUT_DIM,), jnp.float32, -s2, s2)
        g = np.sqrt(6.0 / (OUT_DIM + OUT_DIM))
        Wg = jax.random.uniform(ks[8], (OUT_DIM, OUT_DIM), jnp.float32, -g, g)
        bg = jnp.zeros((OUT_DIM,), dtype=jnp.float32)
        return dict(node_features=node_features, W1=W1, b1=b1, W2=W2, b2=b2, Wg=Wg, bg=bg, edge_src=edge_src, edge_dst=edge_dst, edgetypes=edgetypes)
    _L3_gnn_all = _L3_gnn_setup()
    _L3_gnn_in = {k: v for k, v in _L3_gnn_all.items() if k in ('W1', 'b1', 'W2', 'b2', 'Wg', 'bg')}
    del _L3_gnn_all
    return {'x': x, 'src': src, 'dst': dst, 'edge_attr_3': edge_attr_3, 'edge_type_4': edge_type_4, 'edge_weight': edge_weight, 'L2_gnn_W1': _L2_gnn_in['W1'], 'L2_gnn_R1': _L2_gnn_in['R1'], 'L2_gnn_b1': _L2_gnn_in['b1'], 'L2_gnn_g1': _L2_gnn_in['g1'], 'L2_gnn_be1': _L2_gnn_in['be1'], 'L2_gnn_W2': _L2_gnn_in['W2'], 'L2_gnn_R2': _L2_gnn_in['R2'], 'L2_gnn_b2': _L2_gnn_in['b2'], 'L2_gnn_g2': _L2_gnn_in['g2'], 'L2_gnn_be2': _L2_gnn_in['be2'], 'L2_gnn_W3': _L2_gnn_in['W3'], 'L2_gnn_R3': _L2_gnn_in['R3'], 'L2_gnn_b3': _L2_gnn_in['b3'], 'L2_gnn_g3': _L2_gnn_in['g3'], 'L2_gnn_be3': _L2_gnn_in['be3'], 'L3_gnn_W1': _L3_gnn_in['W1'], 'L3_gnn_b1': _L3_gnn_in['b1'], 'L3_gnn_W2': _L3_gnn_in['W2'], 'L3_gnn_b2': _L3_gnn_in['b2'], 'L3_gnn_Wg': _L3_gnn_in['Wg'], 'L3_gnn_bg': _L3_gnn_in['bg']}

def reference(x, src, dst, edge_attr_3, edge_type_4, edge_weight, L2_gnn_W1, L2_gnn_R1, L2_gnn_b1, L2_gnn_g1, L2_gnn_be1, L2_gnn_W2, L2_gnn_R2, L2_gnn_b2, L2_gnn_g2, L2_gnn_be2, L2_gnn_W3, L2_gnn_R3, L2_gnn_b3, L2_gnn_g3, L2_gnn_be3, L3_gnn_W1, L3_gnn_b1, L3_gnn_W2, L3_gnn_b2, L3_gnn_Wg, L3_gnn_bg):
    import jax
    import jax.numpy as jnp

    def _L0_gnn_ref(x, edge_index, num_layers):
        import jax, jax.numpy as jnp
        import numpy as np
        N_NODES = 6250
        N_EDGES = 100000
        LATENT_DIM = 32
        NUM_LAYERS = 3
        N = x.shape[0]
        src = edge_index[0]
        dst = edge_index[1]
        cnt = jax.ops.segment_sum(jnp.ones((edge_index.shape[1],), x.dtype), dst, num_segments=N)
        denom = jnp.maximum(cnt, 1.0)[:, None]
        scale = 1.0 / (num_layers + 1)
        final = x * scale
        for _ in range(num_layers):
            summed = jax.ops.segment_sum(x[src], dst, num_segments=N)
            x = summed / denom
            final = final + x * scale
        return final

    def _L1_gnn_ref(emb, edge_weight, row, col, num_layers):
        import jax, jax.numpy as jnp
        import numpy as np
        N_NODES = 6250
        N_EDGES = 100000
        EMB_DIM = 32
        NUM_LAYERS = 3
        n = emb.shape[0]
        w = edge_weight[:, None]
        X = emb
        for _ in range(num_layers):
            msgs = w * X[col]
            X = jax.ops.segment_sum(msgs, row, num_segments=n)
        return X

    def _L2_gnn_ref(patch_embs, edge_index, edge_attr, W1, R1, b1, g1, be1, W2, R2, b2, g2, be2, W3, R3, b3, g3, be3):
        import jax, jax.numpy as jnp
        import numpy as np
        N = 3125
        E = 100000
        C = 32
        KS = 4
        DIM = 3
        K3 = KS ** DIM
        NEG = 0.01
        EPS = 1e-05
        _BITS = np.array([[s >> d & 1 for d in range(DIM)] for s in range(2 ** DIM)], dtype=np.int32)

        def _basis(edge_attr):
            v = edge_attr * (KS - 1)
            lo = jnp.floor(v)
            f = v - lo
            lo = lo.astype(jnp.int32)
            bits = jnp.asarray(_BITS)
            idx = jnp.clip(lo[:, None, :] + bits[None], 0, KS - 1)
            w = jnp.where(bits[None] == 1, f[:, None, :], 1.0 - f[:, None, :])
            basis = jnp.prod(w, axis=-1)
            wi = idx[..., 0] + KS * idx[..., 1] + KS * KS * idx[..., 2]
            return (basis, wi)

        def _sconv(x, src, dst, basis, wi, W, R, b):
            n = x.shape[0]
            z = jnp.einsum('nc,kco->nko', x, W)
            msg = jnp.zeros((src.shape[0], W.shape[2]), x.dtype)
            for s in range(basis.shape[1]):
                msg = msg + basis[:, s, None] * z[src, wi[:, s]]
            agg = jax.ops.segment_sum(msg, dst, num_segments=n)
            cnt = jax.ops.segment_sum(jnp.ones((dst.shape[0],), x.dtype), dst, num_segments=n)
            agg = agg / jnp.clip(cnt, 1.0)[:, None]
            return agg + x @ R + b

        def _bn(x, g, be):
            mu = x.mean(0)
            var = x.var(0)
            return (x - mu) * jax.lax.rsqrt(var + EPS) * g + be

        def _leaky(x):
            return jnp.where(x >= 0, x, NEG * x)
        src, dst = (edge_index[0], edge_index[1])
        basis, wi = _basis(edge_attr)
        x = _bn(_leaky(_sconv(patch_embs, src, dst, basis, wi, W1, R1, b1)) + patch_embs, g1, be1)
        x = _bn(_leaky(_sconv(x, src, dst, basis, wi, W2, R2, b2)) + x, g2, be2)
        x = _bn(_sconv(x, src, dst, basis, wi, W3, R3, b3) + x, g3, be3)
        return x

    def _L3_gnn_ref(node_features, W1, b1, W2, b2, Wg, bg, edge_src, edge_dst, edgetypes):
        import jax, jax.numpy as jnp
        import numpy as np
        N_NODES = 6250
        IN_DIM = 32
        ENC_HID = 64
        OUT_DIM = 32
        N_EDGES = 100000

        def _gcn_forward(node_features, W1, b1, W2, b2, Wg, bg, src, dst):
            h0 = jax.nn.relu(node_features @ W1 + b1)
            h0 = jax.nn.relu(h0 @ W2 + b2)
            n = node_features.shape[0]
            loop = jnp.arange(n, dtype=src.dtype)
            s = jnp.concatenate([src, loop])
            d = jnp.concatenate([dst, loop])
            ones = jnp.ones(s.shape[0], dtype=h0.dtype)
            deg_out = jax.ops.segment_sum(ones, s, num_segments=n)
            deg_in = jax.ops.segment_sum(ones, d, num_segments=n)
            norm_src = jax.lax.rsqrt(jnp.clip(deg_out, 1.0))
            norm_dst = jax.lax.rsqrt(jnp.clip(deg_in, 1.0))
            m = (h0 * norm_src[:, None])[s]
            agg = jax.ops.segment_sum(m, d, num_segments=n)
            h1 = agg * norm_dst[:, None] @ Wg + bg
            h1 = jax.nn.relu(h1)
            return h0 + h1
        return _gcn_forward(node_features, W1, b1, W2, b2, Wg, bg, edge_src, edge_dst)
    edge_index = jnp.stack([src, dst])
    h = jnp.maximum(_layernorm(x, axis=-1), 0.0)
    x = x + _L0_gnn_ref(h, edge_index, 3)
    h = jnp.maximum(_layernorm(x, axis=-1), 0.0)
    x = x + _L1_gnn_ref(h, edge_weight, src, dst, 3)
    h = jnp.maximum(_layernorm(x, axis=-1), 0.0)
    x = x + _L2_gnn_ref(h, edge_index, edge_attr_3, L2_gnn_W1, L2_gnn_R1, L2_gnn_b1, L2_gnn_g1, L2_gnn_be1, L2_gnn_W2, L2_gnn_R2, L2_gnn_b2, L2_gnn_g2, L2_gnn_be2, L2_gnn_W3, L2_gnn_R3, L2_gnn_b3, L2_gnn_g3, L2_gnn_be3)
    h = jnp.maximum(_layernorm(x, axis=-1), 0.0)
    x = x + _L3_gnn_ref(h, L3_gnn_W1, L3_gnn_b1, L3_gnn_W2, L3_gnn_b2, L3_gnn_Wg, L3_gnn_bg, src, dst, edge_type_4)
    return x

_drawn_inputs = setup_inputs


def setup_inputs(seed=0):
    import zlib

    import numpy as np

    out = dict(_drawn_inputs(seed))
    spreads = {'L2_gnn_b1': (0.0, 2.0),
     'L2_gnn_g1': (1.0, 0.6),
     'L2_gnn_be1': (0.0, 2.0),
     'L2_gnn_b2': (0.0, 2.0),
     'L2_gnn_g2': (1.0, 0.6),
     'L2_gnn_be2': (0.0, 2.0),
     'L2_gnn_b3': (0.0, 2.0),
     'L2_gnn_g3': (1.0, 0.6),
     'L2_gnn_be3': (0.0, 2.0),
     'L3_gnn_bg': (0.0, 2.0)}
    factors = {'edge_attr_3': 200.0,
     'L2_gnn_W1': 200.0,
     'L2_gnn_R1': 200.0,
     'L2_gnn_W2': 200.0,
     'L2_gnn_R2': 200.0,
     'L2_gnn_W3': 200.0,
     'L2_gnn_R3': 200.0,
     'L3_gnn_W1': 38.126,
     'L3_gnn_b1': 64.0,
     'L3_gnn_W2': 34.464,
     'L3_gnn_b2': 200.0,
     'L3_gnn_Wg': 23.019}
    for name, (base, spread) in spreads.items():
        noise = np.random.default_rng([zlib.crc32(name.encode()), seed]).standard_normal(out[name].shape)
        drawn = base * np.exp(spread * noise) if base else spread * noise
        out[name] = jnp.asarray(drawn.astype(out[name].dtype))
    for name, factor in factors.items():
        out[name] = (out[name] * factor).astype(out[name].dtype)
    return out
```

```python
import concourse.bass as bass
from concourse import mybir
from contextlib import ExitStack

I32, F32, BF16 = mybir.dt.int32, mybir.dt.float32, mybir.dt.bfloat16
ALU = mybir.AluOpType
ACT = mybir.ActivationFunctionType
AX = mybir.AxisListType

N, C, E, HID = 6250, 32, 206250, 64
P = 128
NB = -(-N // P)
NPAD = NB * P
PADNODE = NPAD - 1
TILES = -(-E // P)
T = -(-TILES // P) * P
CHUNKS = T // P
LASTP, LASTN = divmod(E, T)
FULLB, RESTB = divmod(N, P)
REC = 8
DST, SRC, WGT, ATT = 0, 1, 2, 3
UNIT = 8
SETS = 4
BATCH = UNIT * SETS


class Items:
    def __init__(self, shift, ranges):
        self.shift, self.size = shift, 1 << shift
        groups = NPAD >> shift
        self.n = -(-(TILES + groups - 1) // BATCH) * BATCH
        self.ranges, self.width = ranges, self.n // ranges
        self.loops = self.n // BATCH
        self.units = self.n // UNIT


BLK = Items(7, 4)
SPL = Items(3, 5)
K3 = 64
YW = C + 1
SORTS = ((SRC, 7, NB, False), (DST, 3, 32, False), (DST, 8, -(-NPAD >> 8), True))
CONSTS = {}
_at = 0
for _name, _w in (("iota", P), ("ident", P), ("before", P), ("ones", P), ("tile", CHUNKS), ("mask", 1),
                  ("items", SPL.n), ("ident2", C)):
    CONSTS[_name] = (_at, _w)
    _at += _w
CW = _at
WORDS = {}
_at = 0
for _name, _w in (("R1", C), ("R2", C), ("R3", C), ("W1", HID), ("W2", C), ("Wg", C)):
    WORDS[_name] = (_at, _w)
    _at += _w
WW = _at
ROWS = {n: i * C for i, n in enumerate(("g1", "be1", "g2", "be2", "g3", "be3"))}


class Steps:
    def __init__(self, eng, inc, wait=None):
        self.eng, self.inc, self.wait, self.n, self.it, self.start, self.per = eng, inc, wait or inc, 0, 0, 0, 0

    def __call__(self, ins, lag=0):
        ins.then_inc(self.inc, 1)
        self.n += 1
        self.eng.wait_ge(self.wait, self.it * self.per + (self.n - lag))

    def enter(self, it, per, start=0):
        self.at, self.it, self.per, self.start = self.n, it, per, start
        self.n -= start * per

    def leave(self, turns):
        assert self.n - self.at + self.start * self.per == self.per, (self.n, self.at, self.per)
        self.n, self.it, self.per = self.at + turns * self.per, 0, 0


def wait(eng, sem, value):
    if not isinstance(value, int) or value > 0:
        eng.wait_ge(sem, value)


def turns(eng, count, body, peel):
    if peel:
        body(0)
    with eng.Fori(int(peel), count) as it:
        body(it)


def build(nc, ins, out):
    ctx = ExitStack()
    with ctx:
        def sb(name, shape, dt=F32):
            return ctx.enter_context(nc.sbuf_tensor(name, shape, dt))

        def sem(name):
            return ctx.enter_context(nc.semaphore(name))

        def dram(name, shape, dt=F32):
            return nc.dram_tensor(name, shape, dt).ap()

        rec_a = dram("rec_a", (P * T, REC))
        rec_b = dram("rec_b", (P * T, REC))
        rec_c = dram("rec_c", (P * T, REC))
        table = dram("table", (NPAD, C))

        consts = sb("consts", [P, CW])
        iota, ident, before, ones = (consts[:, CONSTS[n][0]:CONSTS[n][0] + P]
                                     for n in ("iota", "ident", "before", "ones"))
        tile_no = consts[:, CONSTS["tile"][0]:CONSTS["tile"][0] + CHUNKS]
        mask = consts[:, CONSTS["mask"][0]:CONSTS["mask"][0] + 1]
        item_no = consts[:, CONSTS["items"][0]:CONSTS["items"][0] + SPL.n]
        ident2 = consts[0:2 * C, CONSTS["ident2"][0]:CONSTS["ident2"][0] + C]
        H = item_no[:, 0:NB * C].rearrange("p (b c) -> p b c", c=C)
        hc = item_no[:, NB * C:NB * C + 7 * C].rearrange("p (b c) -> p b c", c=C)
        wts = sb("wts", [HID + 1, WW])
        bn = sb("bn", [P, 6 * C])

        def W(name):
            a, w = WORDS[name]
            return wts[0:(HID if name == "W2" else C) + 1, a:a + w]

        def row(name):
            return bn[:, ROWS[name]:ROWS[name] + C]

        RAW = 6 * T
        arena = sb("arena", [P, RAW + T * REC])
        raw_d = arena[:, 0:T].bitcast(I32)
        raw_s = arena[:, T:2 * T].bitcast(I32)
        raw_w = arena[:, 2 * T:3 * T]
        raw_a = arena[:, 3 * T:6 * T]
        rec = arena[:, RAW:RAW + T * REC].rearrange("p (t f) -> p t f", f=REC)
        recs = arena[:, RAW:RAW + T * REC].rearrange("p (j e f) -> p j e f", j=CHUNKS, f=REC)
        digit_i = arena[:, 0:T].bitcast(I32)
        digit = arena[:, T:2 * T]
        eqall = arena[:, 2 * T:3 * T]
        emat = arena[:, 0:CHUNKS * SPL.width].rearrange("p (j i) -> p j i", j=CHUNKS)
        emat1 = arena[:, CHUNKS * SPL.width:CHUNKS * SPL.width + SPL.width]
        tileb = arena[:, 8000:8000 + CHUNKS * P].rearrange("p (j e) -> p j e", j=CHUNKS)
        assert CHUNKS * SPL.width + SPL.width <= 8000 and 8000 + CHUNKS * P <= RAW
        MW = UNIT * 2 * P
        mbuf = arena[:, 0:2 * UNIT * P].rearrange("p (m u n) -> p m u n", m=2, u=UNIT)
        pbuf = arena[:, 0:2 * MW].rearrange("p (m u n) -> p m u n", m=2, u=UNIT)
        bbuf = arena[:, 2 * MW:2 * MW + 2 * UNIT * K3].rearrange("p (m u k) -> p m u k", m=2, u=UNIT)
        o = 2 * MW + 2 * UNIT * K3
        ybuf = arena[:, o:o + C * 4 * BATCH].rearrange("p (c i) -> p c i", c=C)
        o += C * 4 * BATCH
        wbd = arena[:, o:o + C * 2 * C].rearrange("p (c n) -> p c n", c=C)
        o += C * 2 * C
        aggt = arena[0:2 * C, o:o + NPAD]
        o += NPAD
        F = arena[:, o:o + NB * C].rearrange("p (b c) -> p b c", c=C)
        o += NB * C
        Y = arena[:, o:o + NB * YW].rearrange("p (b c) -> p b c", c=YW)
        o += NB * YW
        xt = arena[0:C + 1, o:o + 7 * P]
        o += 7 * P
        ht = arena[0:HID + 1, o:o + 7 * P]
        o += 7 * P
        assert o <= RAW + T * REC

        hist = sb("hist", [P, P])
        run = sb("run", [P, P])
        oh = sb("oh", [P, P])
        oh2 = sb("oh2", [P, P])
        tot = sb("tot", [P, 1])
        totb = sb("totb", [P, P])
        posf = sb("posf", [P, 2, UNIT])
        posi = sb("posi", [P, 2, UNIT], I32)
        stage = sb("stage", [P, 2, UNIT * REC])

        c_hi = sb("c_hi", [P, 2, CHUNKS])
        c_i = sb("c_i", [P, 2, CHUNKS], I32)
        c_raw = sb("c_raw", [P, 2, CHUNKS])
        c_prev = sb("c_prev", [P, CHUNKS, 2])
        grp = sb("grp", [P, SPL.width])
        I16 = mybir.dt.int16
        cols16 = sb("cols16", [65, SPL.n], I16)
        by_dst = (sb("dst_row", [P, BLK.n], I16), sb("dst_loc", [P, BLK.n]), None, cols16[0:1, 0:BLK.n])
        by_src = (sb("src_row", [P, BLK.n], I16), sb("src_loc", [P, BLK.n]), sb("src_wgt", [P, BLK.n]), cols16[32:33, 0:BLK.n])
        spl_row = sb("spl_row", [P, SPL.n], I16)
        spl_loc = sb("spl_loc", [P, SPL.n], I16)
        satt = sb("satt", [P, SPL.n, 3])
        scol = cols16[64:65, :]

        idx = sb("idx", [P, SETS, UNIT], I32)
        gat = sb("gat", [P, SETS, UNIT, YW])
        hat = sb("hat", [P, UNIT, 3, 4])
        hat2 = sb("hat2", [P, UNIT, 3, 4])
        pair = sb("pair", [P, UNIT, 4, 4])
        oh8 = sb("oh8", [P, UNIT, 8])

        X = sb("X", [P, NB, C])
        Z = sb("Z", [P, NB, C])
        inv = sb("inv", [P, NB])
        nsrc = sb("nsrc", [P, NB])
        ndst = sb("ndst", [P, NB])
        st = sb("st", [P, NB])
        st2 = sb("st2", [P, NB])
        bst = sb("bst", [P, C])
        bst2 = sb("bst2", [P, C])

        ps = [ctx.enter_context(nc.psum_tensor(f"ps{i}", [P, 512], F32)) for i in range(8)]

        s_const = sem("consts_loaded")
        s_raw_fill = sem("raw_filled")
        s_raw = sem("raw_loaded")
        s_xfill = sem("x_filled")
        s_x = sem("x_and_weights_loaded")
        s_dve = sem("dve_steps")
        s_tope = sem("pe_inputs_ready")
        s_frpe = sem("pe_results_ready")
        s_pos = sem("positions_ready")
        s_staged = sem("records_staged")
        s_scat = [sem(f"records_scattered{h}") for h in range(2)]
        s_resort = sem("records_reloaded")
        s_recs = sem("sorted_records_loaded")
        s_pfill = sem("previous_dst_filled")
        s_prev = sem("previous_dst_loaded")
        s_em = sem("tile_item_matrix")
        s_ex = sem("items_expanded")
        s_wfill = sem("spl_weights_zeroed")
        s_late = sem("spl_weights_loaded")
        s_row = sem("node_rows_ready")
        s_table = sem("node_table_written")
        s_gate = sem("pool_gate")
        s_pegate = sem("pe_gate")
        s_idx = sem("indices_staged")
        s_gat = {kind: [sem(f"rows_gathered_{kind}{m}") for m in range(SETS)] for kind in "AB"}
        a_oh = sem("blk_onehots")
        a_mm = sem("blk_matmuls")
        b_prod = sem("spl_products")
        b_y = sem("spl_y_matmuls")
        b_ev = sem("spl_y_copied")
        b_out = sem("spl_w_matmuls")
        s_sqin = sem("sqrt_inputs")
        s_sqout = sem("sqrt_results")
        s_result = sem("result_ready")
        s_out = sem("output_written")

        block = ctx.enter_context(nc.Block())
        PLAN = ([("A", k, by_dst) for k in range(3)] + [("A", k, by_src) for k in range(3, 6)] +
                [("B", k, None) for k in range(3)] + [("A", 6, by_dst)])
        BUILD = ((BLK, (SRC, DST, WGT)), (BLK, (DST, SRC)), (SPL, (DST, SRC, ATT, ATT + 1, ATT + 2)))
        HALVES = T // UNIT // 2
        SLOT = 16 * UNIT

        def rows(ap):
            return ap.rearrange("(b p) c -> p b c", p=P)

        @block.sync
        def _(sp):
            sp.dma_start(consts[:, :], ins["consts"]).then_inc(s_const, 16)
            sp.wait_ge(s_raw_fill, 1)
            for dst_ap, src_ap, k in ((raw_d, ins["dst"], 1), (raw_s, ins["src"], 1),
                                      (raw_w, ins["edge_weight"], 1), (raw_a, ins["edge_attr_3"], 3)):
                sp.dma_start(dst_ap[0:LASTP, :],
                             src_ap[0:LASTP * T * k].rearrange("(p t) -> p t", p=LASTP)).then_inc(s_raw, 16)
                sp.dma_start(dst_ap[LASTP:LASTP + 1, 0:LASTN * k],
                             src_ap[LASTP * T * k:E * k].rearrange("(p t) -> p t", p=1)).then_inc(s_raw, 16)
            sp.wait_ge(s_xfill, 1)
            sp.dma_start(X[:, 0:FULLB, :], rows(ins["x"][0:FULLB * P, :])).then_inc(s_x, 16)
            sp.dma_start(X[0:RESTB, FULLB, :], ins["x"][FULLB * P:N, :]).then_inc(s_x, 16)
            for name in WORDS:
                r, (a, w) = (HID if name == "W2" else C) + 1, WORDS[name]
                for dst_ap, src_ap in ((wts[0:r - 1, a:a + w], ins[name]), (wts[r - 1:r, a:a + w], ins["b" + name])):
                    sp.dma_start(dst_ap, src_ap).then_inc(s_x, 16)
            for name, a in ROWS.items():
                sp.dma_start(bn[:, a:a + C], ins[name].broadcast_to([P, C])).then_inc(s_x, 16)
            for k in range(3):
                for h in range(2):
                    sp.wait_ge(s_scat[h], SLOT * HALVES * (k + 1))
                if k == 1:
                    sp.dma_start(rec.rearrange("p t f -> p (t f)"),
                                 rec_a.rearrange("(p t) f -> p (t f)", p=P)).then_inc(s_resort, 16)
            sp.wait_ge(s_pfill, 1)
            for k, (sorted_rec, key) in enumerate(((rec_c, SRC), (rec_b, DST))):
                if k:
                    sp.wait_ge(s_ex, BLK.ranges)
                tiles = sorted_rec.rearrange("(j p e) f -> p j e f", p=P, e=P)
                sp.dma_start(recs.rearrange("p j e f -> p j (e f)"), tiles.rearrange("p j e f -> p j (e f)")).then_inc(s_recs, 16)
                last = tiles[:, :, P - 1, 0:2]
                sp.dma_start(c_prev[1:P, :, :], last[0:P - 1, :, :]).then_inc(s_prev, 16)
                sp.dma_start(c_prev[0:1, 1:CHUNKS, :], last[P - 1:P, 0:CHUNKS - 1, :]).then_inc(s_prev, 16)
            sp.wait_ge(s_wfill, 1)
            for n, (kind, k, _) in enumerate(PLAN):
                sp.wait_ge(s_row, n + 1)
                if kind == "B":
                    for j in range(2):
                        sp.dma_start(wbd[K3 * j:K3 * j + K3, :, C * j:C * j + C], ins[f"WS{k + 1}"]).then_inc(s_late, 16)
                sp.dma_start(rows(table), H[:, :, :]).then_inc(s_table, 16)
            sp.wait_ge(s_result, 1)
            sp.dma_start(rows(out[0:FULLB * P, :]), Z[:, 0:FULLB, :]).then_inc(s_out, 16)
            sp.dma_start(out[FULLB * P:N, :], Z[0:RESTB, FULLB, :]).then_inc(s_out, 16)
            sp.wait_ge(s_out, 32)

        @block.gpsimd
        def _(pool):
            for k, dst_rec in enumerate((rec_c, rec_a, rec_b)):
                with pool.Fori(0, HALVES) as it:
                    for h in range(2):
                        pool.wait_ge(s_staged, it * 2 + (2 * HALVES * k + h + 1))
                        pool.sem_inc(s_gate, 1)
                        for u in range(UNIT):
                            pool.indirect_dma_start(
                                out=dst_rec, out_offset=bass.IndirectOffsetOnAxis(ap=posi[:, h, u:u + 1], axis=0),
                                in_=stage[:, h, u * REC:(u + 1) * REC], in_offset=None).then_inc(s_scat[h], 16)
            done = 0
            for n, (kind, k, _) in enumerate(PLAN):
                items = BLK if kind == "A" else SPL
                pool.wait_ge(s_table, 16 * (n + 1))
                pool.sem_inc(s_gate, 1)
                with pool.Fori(0, items.loops) as it:
                    for m in range(SETS):
                        pool.wait_ge(s_idx, it * SETS + (done + m + 1))
                        pool.sem_inc(s_gate, 1)
                        for u in range(UNIT):
                            pool.indirect_dma_start(
                                out=gat[:, m, u, 0:C], out_offset=None, in_=table,
                                in_offset=bass.IndirectOffsetOnAxis(ap=idx[:, m, u:u + 1], axis=0)).then_inc(s_gat[kind][m], 16)
                done += items.units

        @block.scalar
        def _(act):
            sqrt_no = 0

            def sqrts(*pairs):
                nonlocal sqrt_no
                sqrt_no += 1
                act.wait_ge(s_sqin, sqrt_no)
                for dst_ap, src_ap in pairs:
                    last = act.sqrt(dst_ap, src_ap)
                last.then_inc(s_sqout, 1)

            for k in range(3):
                if k == 2:
                    act.wait_ge(s_resort, 16)

                def staging(it):
                    for h in range(2):
                        wait(act, s_scat[h], it * SLOT + SLOT * HALVES * k)
                        act.wait_ge(s_pos, it * 2 + (2 * HALVES * k + h + 1))
                        act.copy(posi[:, h, :], posf[:, h, :])
                        act.copy(stage[:, h, :].rearrange("p (u f) -> p u f", f=REC),
                                 rec[:, bass.ds(it * (2 * UNIT) + h * UNIT, UNIT), :]).then_inc(s_staged, 1)
                turns(act, HALVES, staging, peel=(k == 0))

            for n, (kind, k, tab) in enumerate(PLAN):
                if n in (0, 3, 6, 9):
                    sqrts((st2[:, :], st[:, :]))
                act.wait_ge(s_table, 16 * (n + 1))
                if kind == "A":
                    def stage_a(it):
                        for m in range(SETS):
                            wait(act, a_mm, it * SETS + (k * BLK.units + m + 1 - SETS) if n or not isinstance(it, int) else 0)
                            act.copy(idx[:, m, :], tab[0][:, bass.ds(it * BATCH + m * UNIT, UNIT)]).then_inc(s_idx, 1)
                    turns(act, BLK.loops, stage_a, peel=(n == 0))
                else:
                    ub = k * SPL.units
                    for m in range(SETS):
                        act.copy(idx[:, m, :], spl_row[:, m * UNIT:(m + 1) * UNIT]).then_inc(s_idx, 1)

                    def stage_b(it, more=True):
                        wait(act, b_out, it + k * SPL.loops)
                        for m in range(SETS):
                            act.wait_ge(b_y, it * SETS + (ub + m + 1))
                            for q in range(2):
                                i0 = 16 * (2 * m + q)
                                last = act.copy(ybuf[:, :, i0:i0 + 16].rearrange("p c i -> p i c"),
                                                ps[2 * (m % 2) + q][:, :].rearrange("p (i c) -> p i c", c=C))
                            last.then_inc(b_ev, 1)
                            if more:
                                act.copy(idx[:, m, :], spl_row[:, bass.ds((it + 1) * BATCH + m * UNIT, UNIT)]).then_inc(s_idx, 1)
                    turns(act, SPL.loops - 1, stage_b, peel=(k == 0))
                    stage_b(SPL.loops - 1, more=False)
                    sqrts((bst2[:, :], bst[:, :]))
                if n == 0:
                    sqrts((ndst[:, :], st2[:, :]))
                if n == 3:
                    sqrts((nsrc[:, :], st2[:, :]))

        @block.tensor
        def _(pe):
            asked = 0

            def request(it=0, per=0):
                nonlocal asked
                asked += 1
                pe.wait_ge(s_tope, it * per + asked)

            for _, _, nd, _ in SORTS:
                request()
                pe.matmul(ps[1][0:nd, 0:1], hist[:, 0:nd], ones[:, 0:1], start=True, stop=True).then_inc(s_frpe, 1)
                request()
                pe.matmul(ps[1][:, P:P + nd], before, hist[:, 0:nd], start=True, stop=False)
                pe.matmul(ps[1][:, P:P + nd], totb[0:nd, :], before[0:nd, 0:nd], start=False, stop=True).then_inc(s_frpe, 1)
            n = 0
            for b, (items, fields) in enumerate(BUILD):
                for _ in range(items.ranges):
                    n += 1
                    pe.wait_ge(s_em, n)
                    w = items.width
                    for f, field in enumerate((None,) + fields):
                        for j in range(CHUNKS):
                            lhs = tileb[:, j, :] if field is None else recs[:, j, :, field]
                            mm = pe.matmul(ps[f][:, 0:w], lhs, emat[:, j, 0:w], start=(j == 0), stop=(j == CHUNKS - 1))
                    mm.then_inc(s_ex, 1)

            def linear(name, hidden=False):
                nonlocal asked
                per, base = (3 if hidden else 2), asked
                with pe.Fori(0, 7) as it:
                    asked = base
                    request(it, per)
                    for b in range(7):
                        mm = pe.matmul(ps[b // 4][0:C, (b % 4) * P:(b % 4 + 1) * P], hc[:, b, :], ident, start=True, stop=True)
                    mm.then_inc(s_frpe, 1)
                    request(it, per)
                    if hidden:
                        pe.sem_inc(s_pegate, 1)
                        pe.matmul(ps[0][0:HID, :], W("W1"), xt[:, 0:512], start=True, stop=True)
                        pe.matmul(ps[1][0:HID, 0:384], W("W1"), xt[:, 512:896], start=True, stop=True).then_inc(s_frpe, 1)
                        request(it, per)
                    for b in range(7):
                        mm = pe.matmul(ps[2][:, b * C:(b + 1) * C], (ht if hidden else xt)[:, b * P:(b + 1) * P], W(name),
                                       start=True, stop=True)
                    mm.then_inc(s_frpe, 1)
                asked = base + 7 * per

            for n, (kind, k, _) in enumerate(PLAN):
                gb = SLOT * (k * BLK.loops + 1)
                if n == 9:
                    linear("W2", hidden=True)
                if kind == "A":
                    with pe.Fori(0, BLK.loops) as it:
                        for m in range(SETS):
                            pe.wait_ge(s_gat["A"][m], it * SLOT + gb)
                            pe.wait_ge(a_oh, it * SETS + (k * BLK.units + m + 1))
                            for u in range(UNIT):
                                mm = pe.matmul(ps[m][:, u * YW:(u + 1) * YW], mbuf[:, m % 2, u, :], gat[:, m, u, :],
                                               start=True, stop=True)
                            mm.then_inc(a_mm, 1)
                else:
                    ub = k * SPL.units
                    pe.wait_ge(s_late, 32 * (k + 1))

                    def spline(it):
                        for m in range(SETS):
                            pe.wait_ge(b_prod, it * SETS + (ub + m + 1))
                            if m >= 2 or k or not isinstance(it, int):
                                pe.wait_ge(b_ev, it * SETS + (ub + m - 1))
                            for u in range(UNIT):
                                p0, c0 = K3 * (u % 2), 8 * C * (u // 2 % 2)
                                mm = pe.matmul(ps[2 * (m % 2) + u // 4][p0:p0 + K3, c0:c0 + 8 * C],
                                               bbuf[:, m % 2, u, :], pbuf[:, m % 2, u, :], start=True, stop=True)
                            mm.then_inc(b_y, 1)
                        pe.wait_ge(b_ev, it * SETS + (ub + SETS))
                        for c in range(C):
                            mm = pe.matmul(ps[4][0:2 * C, 0:4 * BATCH], wbd[:, c, :], ybuf[:, c, :], start=(c == 0), stop=(c == C - 1))
                        mm.then_inc(b_out, 1)
                    turns(pe, SPL.loops, spline, peel=(k == 0))
                    request()
                    for t in range(NB):
                        mm = pe.matmul(ps[t // 16][:, (t % 16) * C:(t % 16 + 1) * C], aggt[:, t * P:(t + 1) * P], ident2, start=True, stop=True)
                    mm.then_inc(s_frpe, 1)
                    linear(f"R{k + 1}")
                    for _ in range(2):
                        request()
                        pe.matmul(ps[0][:, 0:C], ones, bst[:, :], start=True, stop=True).then_inc(s_frpe, 1)
            linear("Wg")

        @block.vector
        def _(dve):
            v = nc.vector
            step = Steps(dve, s_dve)
            to_pe = Steps(dve, s_tope, s_frpe)
            to_act = Steps(dve, s_sqin, s_sqout)

            def per_node(ap):
                return ap.unsqueeze(2).to_broadcast([P, NB, C])

            def per_feature(ap):
                return ap.unsqueeze(1).to_broadcast([P, NB, C])

            step(v.memset(raw_d, PADNODE))
            step(v.memset(raw_s, PADNODE))
            step(v.memset(raw_w, 0.0))
            v.memset(raw_a, 0.0).then_inc(s_raw_fill, 1)
            dve.wait_ge(s_raw_fill, 1)
            v.memset(X[:, :, :], 0.0).then_inc(s_xfill, 1)
            v.memset(c_prev[:, :, :], 0.0).then_inc(s_pfill, 1)
            step(v.memset(gat[:, :, :, :], 1.0))
            step(v.memset(rec[:, :, 6:REC], 0.0))
            dve.wait_ge(s_raw, 16 * 8)
            step(v.tensor_copy(rec[:, :, DST], raw_d))
            step(v.tensor_copy(rec[:, :, SRC], raw_s))
            step(v.tensor_copy(rec[:, :, WGT], raw_w))
            step(v.tensor_copy(rec[:, :, ATT:ATT + 3], raw_a.rearrange("p (t f) -> p t f", f=3)))
            dve.wait_ge(s_const, 16)

            for k, (field, shift, nd, more) in enumerate(SORTS):
                if more:
                    dve.wait_ge(s_resort, 16)
                step(v.tensor_copy(digit_i, rec[:, :, field]))
                step(v.tensor_scalar(digit_i, digit_i, shift, None, ALU.logical_shift_right))
                if k == 1:
                    step(v.tensor_scalar(digit_i, digit_i, nd - 1, None, ALU.bitwise_and))
                step(v.tensor_copy(digit, digit_i))
                with dve.Fori(0, nd) as d:
                    step.enter(d, 2)
                    step(v.tensor_scalar(eqall, digit, iota[:, bass.ds(d, 1)], None, ALU.is_equal))
                    step(v.tensor_reduce(hist[:, bass.ds(d, 1)], eqall, AX.X, ALU.add))
                    step.leave(nd)
                to_pe(v.memset(tot[:, :], 0.0))
                step(v.tensor_copy(tot[0:nd, :], ps[1][0:nd, 0:1]))
                to_pe(v.tensor_copy(totb[0:nd, :], tot[0:nd, :].to_broadcast([nd, P])))
                step(v.tensor_copy(run[:, 0:nd], ps[1][:, P:P + nd]))

                def positions(it):
                    for h in range(2):
                        wait(dve, s_staged, it * 2 + (2 * HALVES * k + h - 1) if k or not isinstance(it, int) else 0)
                        for u in range(UNIT):
                            col = it * (2 * UNIT) + (h * UNIT + u)
                            step(v.tensor_scalar(oh[:, 0:nd], iota[:, 0:nd], digit[:, bass.ds(col, 1)], None, ALU.is_equal))
                            step(v.tensor_tensor_reduce(out=oh2[:, 0:nd], in0=oh[:, 0:nd], in1=run[:, 0:nd], scale=1.0, scalar=0.0,
                                                        op0=ALU.mult, op1=ALU.add, accum_out=posf[:, h, u:u + 1]))
                            add = v.tensor_tensor(run[:, 0:nd], run[:, 0:nd], oh[:, 0:nd], ALU.add)
                            if u < UNIT - 1:
                                step(add)
                            else:
                                add.then_inc(s_pos, 1)
                                dve.wait_ge(s_pos, it * 2 + (2 * HALVES * k + h + 1))
                per = 2 * (3 * UNIT - 1)
                peeled = int(k == 0)
                if peeled:
                    positions(0)
                with dve.Fori(peeled, HALVES) as it:
                    step.enter(it, per, peeled)
                    positions(it)
                    step.leave(HALVES - peeled)

            for j in range(CHUNKS):
                last = v.tensor_copy(tileb[:, j, :], tile_no[:, j:j + 1].to_broadcast([P, P]))
            step(last)
            n = 0
            for b, (items, fields) in enumerate(BUILD):
                if b < 2:
                    dve.wait_ge(s_recs, 16 * (b + 1))
                    dve.wait_ge(s_prev, 32 * (b + 1))
                step(v.tensor_copy(c_i[:, 0, :], recs[:, :, P - 1, fields[0]]))
                step(v.tensor_copy(c_i[:, 1, :], c_prev[:, :, fields[0]]))
                step(v.tensor_scalar(c_i[:, :, :], c_i[:, :, :], items.shift, None, ALU.logical_shift_right))
                step(v.tensor_copy(c_hi[:, :, :], c_i[:, :, :]))
                step(v.tensor_tensor(c_hi[:, 0, :], c_hi[:, 0, :], tile_no, ALU.add))
                step(v.tensor_tensor(c_hi[:, 1, :], c_hi[:, 1, :], tile_no, ALU.add))
                step(v.tensor_scalar(c_hi[:, 1, :], c_hi[:, 1, :], -1.0, None, ALU.add))
                for r in range(items.ranges):
                    w, a = items.width, r * items.width
                    nos = item_no[:, a:a + w]
                    n += 1
                    for j in range(CHUNKS):
                        step(v.tensor_scalar(emat1[:, 0:w], nos, c_hi[:, 0, j:j + 1], None, ALU.is_le))
                        last = v.scalar_tensor_tensor(emat[:, j, 0:w], nos, c_hi[:, 1, j:j + 1], emat1[:, 0:w], ALU.is_gt, ALU.mult)
                        if j < CHUNKS - 1:
                            step(last)
                    last.then_inc(s_em, 1)
                    dve.wait_ge(s_em, n)
                    dve.wait_ge(s_ex, n)
                    step(v.tensor_tensor(grp[:, 0:w], nos, ps[0][:, 0:w], ALU.subtract))
                    table_row, loc, wgt, col = (by_src, by_dst, (spl_row, spl_loc, None, scol))[b]
                    part = 32 * (1, 0, 2)[b]
                    step(v.scalar_tensor_tensor(loc[:, a:a + w], grp[:, 0:w], -float(items.size), ps[1][:, 0:w], ALU.mult, ALU.add))
                    step(v.tensor_copy(table_row[:, a:a + w], ps[2][:, 0:w]))
                    step(v.tensor_scalar(col[:, a:a + w], grp[part:part + 1, 0:w], float(YW if items is BLK else SPL.size), None, ALU.mult))
                    if wgt is not None:
                        step(v.tensor_copy(wgt[:, a:a + w], ps[3][:, 0:w]))
                    if items is SPL:
                        for d in range(3):
                            step(v.tensor_scalar(satt[:, a:a + w, d], ps[3 + d][:, 0:w], 3.0, 0.0, ALU.mult, ALU.max))
                            step(v.tensor_scalar(satt[:, a:a + w, d], satt[:, a:a + w, d], 3.0, None, ALU.min))
            step(v.memset(ht, 1.0))
            step(v.memset(xt, 1.0))
            v.memset(wbd, 0.0).then_inc(s_wfill, 1)
            dve.wait_ge(s_wfill, 1)
            dve.wait_ge(s_x, 16 * (2 + 2 * len(WORDS) + len(ROWS)))

            def layernorm_relu():
                step(v.tensor_reduce(st[:, :], X[:, :, :], AX.X, ALU.add))
                step(v.tensor_scalar(st[:, :], st[:, :], -1.0 / C, None, ALU.mult))
                step(v.tensor_tensor(Z[:, :, :], X[:, :, :], per_node(st[:, :]), ALU.add))
                step(v.tensor_tensor(H[:, :, :], Z[:, :, :], Z[:, :, :], ALU.mult))
                step(v.tensor_reduce(st[:, :], H[:, :, :], AX.X, ALU.add))
                to_act(v.tensor_scalar(st[:, :], st[:, :], 1.0 / C, 1e-5, ALU.mult, ALU.add))
                step(v.reciprocal(st2[:, :], st2[:, :]))
                step(v.tensor_tensor(H[:, :, :], Z[:, :, :], per_node(st2[:, :]), ALU.mult))
                return v.tensor_scalar(H[:, :, :], H[:, :, :], 0.0, None, ALU.max)

            def send_rows(n, ins_):
                ins_.then_inc(s_row, 1)
                dve.wait_ge(s_row, n + 1)

            col_regs = [dve.alloc_register(f"column{u}") for u in range(UNIT)]

            def columns(tab, at, most):
                dve.load(col_regs, tab[0:1, bass.ds(at, UNIT)])
                return [dve.snap(r, min_val=0, max_val=most) for r in col_regs]

            def propagate(k, tab):
                _, loc, wgt, col = tab
                step(v.memset(Y[:, :, :], 0.0))
                yflat = Y[:, :, :].rearrange("p b c -> p (b c)")
                with dve.Fori(0, BLK.loops) as it:
                    step.enter(it, SETS * UNIT)
                    for m in range(SETS):
                        for u in range(UNIT):
                            i = bass.ds(it * BATCH + (m * UNIT + u), 1)
                            last = v.tensor_scalar(mbuf[:, m % 2, u, :], iota, loc[:, i], None, ALU.is_equal)
                        if wgt is not None:
                            dve.wait_ge(s_gat["A"][m], it * SLOT + SLOT * (k * BLK.loops + 1))
                            at = bass.ds(it * BATCH + m * UNIT, UNIT)
                            last = v.tensor_tensor(gat[:, m, :, 0:C], gat[:, m, :, 0:C],
                                                   wgt[:, at].unsqueeze(2).to_broadcast([P, UNIT, C]), ALU.mult)
                        last.then_inc(a_oh, 1)
                        cols = columns(col, it * BATCH + m * UNIT, (NB - 1) * YW)
                        dve.wait_ge(a_mm, it * SETS + (k * BLK.units + m + 1))
                        for u in range(UNIT):
                            dst_ap = yflat[:, bass.ds(cols[u], YW)]
                            step(v.tensor_tensor(dst_ap, dst_ap, ps[m][:, u * YW:(u + 1) * YW], ALU.add))
                    step.leave(BLK.loops)

            def spline(n, k):
                gb, ub = SLOT * (k * SPL.loops + 1), k * SPL.units
                step(v.memset(aggt, 0.0))

                def products(it, m):
                    at = bass.ds(it * BATCH + m * UNIT, UNIT)
                    step(v.tensor_tensor(hat[:, :, :, :], satt[:, at, :].unsqueeze(3).to_broadcast([P, UNIT, 3, 4]),
                                         iota[:, 0:4].unsqueeze(1).unsqueeze(1).to_broadcast([P, UNIT, 3, 4]), ALU.subtract))
                    step(v.scalar_tensor_tensor(hat2[:, :, :, :], hat[:, :, :, :], -1.0, hat[:, :, :, :], ALU.mult, ALU.min))
                    step(v.tensor_scalar(hat[:, :, :, :], hat2[:, :, :, :], 1.0, 0.0, ALU.add, ALU.max))
                    step(v.tensor_tensor(pair[:, :, :, :], hat[:, :, 1, :].unsqueeze(3).to_broadcast([P, UNIT, 4, 4]),
                                         hat[:, :, 0, :].unsqueeze(2).to_broadcast([P, UNIT, 4, 4]), ALU.mult))
                    step(v.tensor_tensor(oh8[:, :, :], iota[:, 0:8].unsqueeze(1).to_broadcast([P, UNIT, 8]),
                                         spl_loc[:, at].unsqueeze(2).to_broadcast([P, UNIT, 8]), ALU.is_equal))
                    if m >= 2 or k or not isinstance(it, int):
                        dve.wait_ge(b_y, it * SETS + (ub + m - 1))
                    step(v.tensor_tensor(bbuf[:, m % 2, :, :].rearrange("p u (a b) -> p u a b", a=4),
                                         hat[:, :, 2, :].unsqueeze(3).to_broadcast([P, UNIT, 4, 16]),
                                         pair[:, :, :, :].rearrange("p u a b -> p u (a b)").unsqueeze(2).to_broadcast([P, UNIT, 4, 16]), ALU.mult))
                    dve.wait_ge(s_gat["B"][m], it * SLOT + gb)
                    v.tensor_tensor(pbuf[:, m % 2, :, :].rearrange("p u (j c) -> p u j c", j=8),
                                    oh8[:, :, :].unsqueeze(3).to_broadcast([P, UNIT, 8, C]),
                                    gat[:, m, :, 0:C].unsqueeze(2).to_broadcast([P, UNIT, 8, C]), ALU.mult).then_inc(b_prod, 1)
                    dve.wait_ge(b_prod, it * SETS + (ub + m + 1))

                def sums(it):
                    dve.wait_ge(b_out, it + (k * SPL.loops + 1))
                    for m in range(SETS):
                        cols = columns(scol, it * BATCH + m * UNIT, NPAD - SPL.size)
                        for u in range(UNIT):
                            p0, i = C * (u % 2), SPL.size * (m * UNIT // 2 + u // 2)
                            dst_ap = aggt[p0:p0 + C, bass.ds(cols[u], SPL.size)]
                            step(v.tensor_tensor(dst_ap, dst_ap, ps[4][p0:p0 + C, i:i + SPL.size], ALU.add),
                                 lag=int(u < UNIT - 1))

                for m in range(SETS):
                    products(0, m)
                with dve.Fori(1, SPL.loops) as it:
                    step.enter(it, SETS * 6 + BATCH, 1)
                    products(it, 0)
                    products(it, 1)
                    sums(it - 1)
                    products(it, 2)
                    products(it, 3)
                    step.leave(SPL.loops - 1)
                sums(SPL.loops - 1)

            def linear(dst_ap, hidden=False):
                with dve.Fori(0, 7) as it:
                    step.enter(it, 2 + hidden)
                    to_pe.enter(it, 2 + hidden)
                    to_pe(v.tensor_copy(hc[:, :, :], H[:, bass.ds(it * 7, 7), :]))
                    step(v.tensor_copy(xt[0:C, 0:512], ps[0][0:C, :]))
                    to_pe(v.tensor_copy(xt[0:C, 512:896], ps[1][0:C, 0:384]))
                    if hidden:
                        step(v.tensor_scalar(ht[0:HID, 0:512], ps[0][0:HID, :], 0.0, None, ALU.max))
                        to_pe(v.tensor_scalar(ht[0:HID, 512:896], ps[1][0:HID, 0:384], 0.0, None, ALU.max))
                    step(v.tensor_copy(dst_ap[:, bass.ds(it * 7, 7), :], ps[2][:, 0:7 * C].rearrange("p (b c) -> p b c", c=C)))
                    step.leave(7)
                    to_pe.leave(7)

            def mask_padding():
                step(v.tensor_scalar(Z[:, NB - 1, :], Z[:, NB - 1, :], mask, None, ALU.mult))

            def convolve(n, k):
                spline(n, k)
                to_pe(v.memset(tot[:, :], 0.0))
                for t in range(4):
                    b0, nb = 16 * t, min(16, NB - 16 * t)
                    step(v.tensor_tensor(Z[:, b0:b0 + nb, :], ps[t][:, 0:nb * C].rearrange("p (b c) -> p b c", c=C),
                                         inv[:, b0:b0 + nb].unsqueeze(2).to_broadcast([P, nb, C]), ALU.mult))
                linear(F)
                step(v.tensor_tensor(Z[:, :, :], Z[:, :, :], F[:, :, :], ALU.add))
                if k < 2:
                    step(v.tensor_scalar(F[:, :, :], Z[:, :, :], 0.01, None, ALU.mult))
                    step(v.tensor_tensor(Z[:, :, :], Z[:, :, :], F[:, :, :], ALU.max))
                step(v.tensor_tensor(Z[:, :, :], Z[:, :, :], H[:, :, :], ALU.add))
                mask_padding()
                to_pe(v.tensor_reduce(bst[:, :], Z[:, :, :].rearrange("p b c -> p c b"), AX.X, ALU.add))
                step(v.tensor_scalar(bst2[:, :], ps[0][:, 0:C], -1.0 / N, None, ALU.mult))
                step(v.tensor_tensor(Z[:, :, :], Z[:, :, :], per_feature(bst2[:, :]), ALU.add))
                mask_padding()
                step(v.tensor_tensor(F[:, :, :], Z[:, :, :], Z[:, :, :], ALU.mult))
                to_pe(v.tensor_reduce(bst[:, :], F[:, :, :].rearrange("p b c -> p c b"), AX.X, ALU.add))
                to_act(v.tensor_scalar(bst[:, :], ps[0][:, 0:C], 1.0 / N, 1e-5, ALU.mult, ALU.add))
                step(v.reciprocal(bst2[:, :], bst2[:, :]))
                step(v.tensor_tensor(bst2[:, :], bst2[:, :], row(f"g{k + 1}"), ALU.mult))
                step(v.tensor_tensor(H[:, :, :], Z[:, :, :], per_feature(bst2[:, :]), ALU.mult))
                return v.tensor_tensor(H[:, :, :], H[:, :, :], per_feature(row(f"be{k + 1}")), ALU.add)

            send_rows(0, layernorm_relu())
            step(v.tensor_scalar(F[:, :, :], H[:, :, :], 0.25, None, ALU.mult))
            for k in range(3):
                propagate(k, by_dst)
                if k == 0:
                    to_act(v.tensor_scalar(st2[:, :], Y[:, :, C], 1.0, 1.0, ALU.add, ALU.max))
                    step(v.tensor_scalar(inv[:, :], Y[:, :, C], 1.0, None, ALU.max))
                    step(v.reciprocal(inv[:, :], inv[:, :]))
                    step(v.reciprocal(ndst[:, :], ndst[:, :]))
                mean = v.tensor_tensor(H[:, :, :], Y[:, :, 0:C], per_node(inv[:, :]), ALU.mult)
                if k < 2:
                    send_rows(k + 1, mean)
                else:
                    step(mean)
                step(v.tensor_scalar(Z[:, :, :], H[:, :, :], 0.25, None, ALU.mult))
                step(v.tensor_tensor(F[:, :, :], F[:, :, :], Z[:, :, :], ALU.add))
            step(v.tensor_tensor(X[:, :, :], X[:, :, :], F[:, :, :], ALU.add))
            send_rows(3, layernorm_relu())
            for k in range(3, 6):
                propagate(k, by_src)
                if k == 3:
                    to_act(v.tensor_scalar(st2[:, :], Y[:, :, C], 1.0, 1.0, ALU.add, ALU.max))
                    step(v.reciprocal(nsrc[:, :], nsrc[:, :]))
                if k < 5:
                    send_rows(k + 1, v.tensor_copy(H[:, :, :], Y[:, :, 0:C]))
            step(v.tensor_tensor(X[:, :, :], X[:, :, :], Y[:, :, 0:C], ALU.add))
            send_rows(6, layernorm_relu())
            for k in range(3):
                last = convolve(6 + k, k)
                if k < 2:
                    send_rows(7 + k, last)
                else:
                    step(last)
            step(v.tensor_tensor(X[:, :, :], X[:, :, :], H[:, :, :], ALU.add))
            step(layernorm_relu())
            linear(F, hidden=True)
            step(v.tensor_scalar(F[:, :, :], F[:, :, :], 0.0, None, ALU.max))
            send_rows(9, v.tensor_tensor(H[:, :, :], F[:, :, :], per_node(nsrc[:, :]), ALU.mult))
            propagate(6, by_dst)
            step(v.tensor_tensor(H[:, :, :], Y[:, :, 0:C], H[:, :, :], ALU.add))
            step(v.tensor_tensor(H[:, :, :], H[:, :, :], per_node(ndst[:, :]), ALU.mult))
            linear(Z)
            step(v.tensor_scalar(Z[:, :, :], Z[:, :, :], 0.0, None, ALU.max))
            step(v.tensor_tensor(Z[:, :, :], Z[:, :, :], F[:, :, :], ALU.add))
            v.tensor_tensor(Z[:, :, :], Z[:, :, :], X[:, :, :], ALU.add).then_inc(s_result, 1)


def kernel(**inputs):
    import numpy as np
    import concourse.bacc as bacc
    from concourse.bass_utils import run_bass_kernel_spmd as run

    nc = bacc.Bacc("TRN2", target_bir_lowering=False, num_devices=1)
    p = np.arange(P)
    consts = np.zeros((P, CW), np.float32)
    for name, value in (("iota", p[None, :]), ("ident", np.eye(P)), ("before", p[:, None] < p[None, :]), ("ones", 1.0),
                        ("tile", np.arange(CHUNKS)[None, :] * P + p[:, None]),
                        ("mask", ((NB - 1) * P + p < N)[:, None]), ("items", np.arange(SPL.n)[None, :]),
                        ("ident2", p[:, None] % C == np.arange(C)[None, :])):
        a, w = CONSTS[name]
        consts[:, a:a + w] = value
    flat = lambda name: np.ascontiguousarray(inputs[name]).reshape(-1)
    mat = lambda name: np.ascontiguousarray(inputs[name])
    vec = lambda name: np.ascontiguousarray(inputs[name]).reshape(1, -1)
    arrays = {"consts": consts, "x": mat("x"), "src": flat("src"), "dst": flat("dst"),
              "edge_weight": flat("edge_weight"), "edge_attr_3": flat("edge_attr_3")}
    for k in (1, 2, 3):
        arrays[f"WS{k}"] = mat(f"L2_gnn_W{k}")
        arrays[f"R{k}"], arrays[f"bR{k}"] = mat(f"L2_gnn_R{k}"), vec(f"L2_gnn_b{k}")
        arrays[f"g{k}"], arrays[f"be{k}"] = vec(f"L2_gnn_g{k}"), vec(f"L2_gnn_be{k}")
    for w, b in (("W1", "b1"), ("W2", "b2"), ("Wg", "bg")):
        arrays[w], arrays["b" + w] = mat("L3_gnn_" + w), vec("L3_gnn_" + b)
    ins = {name: nc.dram_tensor(f"in_{name}", a.shape, mybir.dt.from_np(a.dtype), kind="ExternalInput").ap()
           for name, a in arrays.items()}
    out = nc.dram_tensor("out", (N, C), F32, kind="ExternalOutput").ap()
    build(nc, ins, out)
    r = run(nc, [{f"in_{name}": a for name, a in arrays.items()}], core_ids=[0])
    return r.results[0]["out"]
```

```python
import concourse.bass as bass
from concourse import mybir
from contextlib import ExitStack

I32, I16, F32 = mybir.dt.int32, mybir.dt.int16, mybir.dt.float32
ALU = mybir.AluOpType
ACT = mybir.ActivationFunctionType
AX = mybir.AxisListType

N, C, E, HID = 6250, 32, 206250, 64
P = 128
NB = -(-N // P)
NPAD = NB * P
PADNODE = NPAD - 1
TILES = -(-E // P)
T = -(-TILES // P) * P
CHUNKS = T // P
LASTP, LASTN = divmod(E, T)
FULLB, RESTB = divmod(N, P)
REC = 8
DST, SRC, WGT, ATT = 0, 1, 2, 3
UNIT = 8
SETS = 4
BATCH = UNIT * SETS


class Items:
    def __init__(self, shift, ranges):
        self.shift, self.size = shift, 1 << shift
        self.groups = groups = NPAD >> shift
        self.n = -(-(TILES + groups - 1) // BATCH) * BATCH
        self.ranges, self.width = ranges, self.n // ranges
        self.loops = self.n // BATCH
        self.units = self.n // UNIT

    def chunks(self, r):
        a = r * self.width
        return range(max(0, a - self.groups + 1) // P, min(T - 1, a + self.width - 1) // P + 1)


BLK = Items(7, 4)
SPL = Items(3, 5)
K3 = 64
YW = C + 1
SORTS = ((SRC, 7, NB, False), (DST, 3, 32, False), (DST, 8, -(-NPAD >> 8), True))
CONSTS = {}
_at = 0
for _name, _w in (("iota", P), ("ident", P), ("before", P), ("ones", P), ("tile", CHUNKS), ("mask", 1),
                  ("items", SPL.n), ("ident2", C)):
    CONSTS[_name] = (_at, _w)
    _at += _w
CW = _at
WORDS = {}
_at = 0
for _name, _w in (("R1", C), ("R2", C), ("R3", C), ("W1", HID), ("W2", C), ("Wg", C)):
    WORDS[_name] = (_at, _w)
    _at += _w
WW = _at
ROWS = {n: i * C for i, n in enumerate(("g1", "be1", "g2", "be2", "g3", "be3"))}


class Steps:
    def __init__(self, eng, inc, wait=None):
        self.eng, self.inc, self.wait, self.n, self.it, self.start, self.per = eng, inc, wait or inc, 0, 0, 0, 0

    def __call__(self, ins, lag=0):
        ins.then_inc(self.inc, 1)
        self.n += 1
        self.eng.wait_ge(self.wait, self.it * self.per + (self.n - lag))

    def enter(self, it, per, start=0):
        self.at, self.it, self.per, self.start = self.n, it, per, start
        self.n -= start * per

    def leave(self, turns):
        assert self.n - self.at + self.start * self.per == self.per, (self.n, self.at, self.per)
        self.n, self.it, self.per = self.at + turns * self.per, 0, 0


def wait(eng, sem, value):
    if not isinstance(value, int) or value > 0:
        eng.wait_ge(sem, value)


def turns(eng, count, body, peel):
    if peel:
        body(0)
    with eng.Fori(int(peel), count) as it:
        body(it)


def build(nc, ins, out):
    ctx = ExitStack()
    with ctx:
        def sb(name, shape, dt=F32):
            return ctx.enter_context(nc.sbuf_tensor(name, shape, dt))

        def sem(name):
            return ctx.enter_context(nc.semaphore(name))

        def dram(name, shape, dt=F32):
            return nc.dram_tensor(name, shape, dt).ap()

        rec_a = dram("rec_a", (P * T, REC))
        rec_b = dram("rec_b", (P * T, REC))
        rec_c = dram("rec_c", (P * T, REC))
        table = dram("table", (NPAD, C))

        consts = sb("consts", [P, CW])
        iota, ident, before, ones = (consts[:, CONSTS[n][0]:CONSTS[n][0] + P]
                                     for n in ("iota", "ident", "before", "ones"))
        tile_no = consts[:, CONSTS["tile"][0]:CONSTS["tile"][0] + CHUNKS]
        mask = consts[:, CONSTS["mask"][0]:CONSTS["mask"][0] + 1]
        item_no = consts[:, CONSTS["items"][0]:CONSTS["items"][0] + SPL.n]
        ident2 = consts[0:2 * C, CONSTS["ident2"][0]:CONSTS["ident2"][0] + C]
        H = item_no[:, 0:NB * C].rearrange("p (b c) -> p b c", c=C)
        hc = item_no[:, NB * C:NB * C + 7 * C].rearrange("p (b c) -> p b c", c=C)
        wts = sb("wts", [HID + 1, WW])
        bn = sb("bn", [P, 6 * C])

        def W(name):
            a, w = WORDS[name]
            return wts[0:(HID if name == "W2" else C) + 1, a:a + w]

        def row(name):
            return bn[:, ROWS[name]:ROWS[name] + C]

        RAW = 6 * T
        arena = sb("arena", [P, RAW + T * REC])
        raw_d = arena[:, 0:T].bitcast(I32)
        raw_s = arena[:, T:2 * T].bitcast(I32)
        raw_w = arena[:, 2 * T:3 * T]
        raw_a = arena[:, 3 * T:6 * T]
        rec = arena[:, RAW:RAW + T * REC].rearrange("p (t f) -> p t f", f=REC)
        recs = arena[:, RAW:RAW + T * REC].rearrange("p (j e f) -> p j e f", j=CHUNKS, f=REC)
        digit_i = arena[:, 0:T].bitcast(I32)
        digit = arena[:, T:2 * T]
        eqall = arena[:, 2 * T:3 * T]
        emat = arena[:, 0:CHUNKS * SPL.width].rearrange("p (j i) -> p j i", j=CHUNKS)
        emat1 = arena[:, CHUNKS * SPL.width:CHUNKS * SPL.width + SPL.width]
        tileb = arena[:, 8000:8000 + CHUNKS * P].rearrange("p (j e) -> p j e", j=CHUNKS)
        assert CHUNKS * SPL.width + SPL.width <= 8000 and 8000 + CHUNKS * P <= RAW
        MW = UNIT * 2 * P
        mbuf = arena[:, 0:2 * UNIT * P].rearrange("p (m u n) -> p m u n", m=2, u=UNIT)
        pbuf = arena[:, 0:2 * MW].rearrange("p (m u n) -> p m u n", m=2, u=UNIT)
        bbuf = arena[:, 2 * MW:2 * MW + 2 * UNIT * K3].rearrange("p (m u k) -> p m u k", m=2, u=UNIT)
        o = 2 * MW + 2 * UNIT * K3
        ybuf = arena[:, o:o + C * 4 * BATCH].rearrange("p (c i) -> p c i", c=C)
        o += C * 4 * BATCH
        wbd = arena[:, o:o + C * 2 * C].rearrange("p (c n) -> p c n", c=C)
        o += C * 2 * C
        aggt = arena[0:2 * C, o:o + NPAD]
        o += NPAD
        F = arena[:, o:o + NB * C].rearrange("p (b c) -> p b c", c=C)
        o += NB * C
        Y = arena[:, o:o + NB * YW].rearrange("p (b c) -> p b c", c=YW)
        o += NB * YW
        xt = arena[0:C + 1, o:o + 7 * P]
        o += 7 * P
        ht = arena[0:HID + 1, o:o + 7 * P]
        o += 7 * P
        assert o <= RAW + T * REC

        nxt = sb("nxt", [P, 2], I32)
        falls = sb("falls", [P, 2])
        flag = sb("flag", [1, 1], I32)
        hist = sb("hist", [P, P])
        run = sb("run", [P, P])
        oh = sb("oh", [P, P])
        oh2 = sb("oh2", [P, P])
        tot = sb("tot", [P, 1])
        totb = sb("totb", [P, P])
        posf = sb("posf", [P, 2, UNIT])
        posi = sb("posi", [P, 2, UNIT], I32)
        stage = sb("stage", [P, 2, UNIT * REC])

        c_hi = sb("c_hi", [P, 2, CHUNKS])
        c_i = sb("c_i", [P, 2, CHUNKS], I32)
        c_prev = sb("c_prev", [P, CHUNKS, 2])
        grp = sb("grp", [P, SPL.width])
        cols16 = sb("cols16", [65, SPL.n], I16)
        by_dst = (sb("dst_row", [P, BLK.n], I16), sb("dst_loc", [P, BLK.n]), None, cols16[0:1, 0:BLK.n])
        by_src = (sb("src_row", [P, BLK.n], I16), sb("src_loc", [P, BLK.n]), sb("src_wgt", [P, BLK.n]), cols16[32:33, 0:BLK.n])
        spl_row = sb("spl_row", [P, SPL.n], I16)
        spl_loc = sb("spl_loc", [P, SPL.n], I16)
        satt = sb("satt", [P, SPL.n, 3])
        scol = cols16[64:65, :]

        idx = sb("idx", [P, SETS, UNIT], I32)
        gat = sb("gat", [P, SETS, UNIT, YW])
        hat = sb("hat", [P, UNIT, 3, 4])
        hat2 = sb("hat2", [P, UNIT, 3, 4])
        pair = sb("pair", [P, UNIT, 4, 4])
        oh8 = sb("oh8", [P, UNIT, 8])

        X = sb("X", [P, NB, C])
        Z = sb("Z", [P, NB, C])
        inv = sb("inv", [P, NB])
        nsrc = sb("nsrc", [P, NB])
        ndst = sb("ndst", [P, NB])
        st = sb("st", [P, NB])
        st2 = sb("st2", [P, NB])
        bst = sb("bst", [P, C])
        bst2 = sb("bst2", [P, C])

        ps = [ctx.enter_context(nc.psum_tensor(f"ps{i}", [P, 512], F32)) for i in range(8)]

        s_const = sem("consts_loaded")
        s_raw_fill = sem("raw_filled")
        s_raw = sem("raw_loaded")
        s_xfill = sem("x_filled")
        s_x = sem("x_and_weights_loaded")
        s_dve = sem("dve_steps")
        s_tope = sem("pe_inputs_ready")
        s_frpe = sem("pe_results_ready")
        s_pos = sem("positions_ready")
        s_staged = sem("records_staged")
        s_scat = [sem(f"records_scattered{h}") for h in range(2)]
        s_flagged = sem("flag_ready")
        d_dve = sem("dst_sort_steps")
        d_tope = sem("dst_sort_pe_inputs")
        d_frpe = sem("dst_sort_pe_results")
        d_pos = sem("dst_sort_positions")
        d_staged = sem("dst_sort_staged")
        d_scat = [sem(f"dst_sort_scattered{h}") for h in range(2)]
        s_next = sem("next_dst_loaded")
        s_packed = sem("records_packed")
        s_copied = sem("records_copied")
        s_resort = sem("records_reloaded")
        s_recs = sem("sorted_records_loaded")
        s_pfill = sem("previous_dst_filled")
        s_prev = sem("previous_dst_loaded")
        s_em = sem("tile_item_matrix")
        s_ex = sem("items_expanded")
        s_wfill = sem("spl_weights_zeroed")
        s_late = sem("spl_weights_loaded")
        s_row = sem("node_rows_ready")
        s_table = sem("node_table_written")
        s_gate = sem("pool_gate")
        s_pegate = sem("pe_gate")
        s_idx = sem("indices_staged")
        s_gat = {kind: [sem(f"rows_gathered_{kind}{m}") for m in range(SETS)] for kind in "AB"}
        a_oh = sem("blk_onehots")
        a_mm = sem("blk_matmuls")
        b_prod = sem("spl_products")
        b_y = sem("spl_y_matmuls")
        b_ev = sem("spl_y_copied")
        b_out = sem("spl_w_matmuls")
        s_sqin = sem("sqrt_inputs")
        s_sqout = sem("sqrt_results")
        s_result = sem("result_ready")
        s_out = sem("output_written")

        block = ctx.enter_context(nc.Block())
        PLAN = ([("A", k, by_dst) for k in range(3)] + [("A", k, by_src) for k in range(3, 6)] +
                [("B", k, None) for k in range(3)] + [("A", 6, by_dst)])
        BUILD = ((BLK, (SRC, DST, WGT)), (BLK, (DST, SRC)), (SPL, (DST, SRC, ATT, ATT + 1, ATT + 2)))
        HALVES = T // UNIT // 2
        SLOT = 16 * UNIT

        def rows(ap):
            return ap.rearrange("(b p) c -> p b c", p=P)

        def is_unsorted(eng):
            eng.wait_ge(s_flagged, 1)
            return eng.value_load(flag[0:1, 0:1], min_val=0, max_val=P * T) > 0

        @block.sync
        def _(sp):
            sp.dma_start(consts[:, :], ins["consts"]).then_inc(s_const, 16)
            sp.wait_ge(s_raw_fill, 1)
            for dst_ap, src_ap, k in ((raw_d, ins["dst"], 1), (raw_s, ins["src"], 1),
                                      (raw_w, ins["edge_weight"], 1), (raw_a, ins["edge_attr_3"], 3)):
                sp.dma_start(dst_ap[0:LASTP, :],
                             src_ap[0:LASTP * T * k].rearrange("(p t) -> p t", p=LASTP)).then_inc(s_raw, 16)
                sp.dma_start(dst_ap[LASTP:LASTP + 1, 0:LASTN * k],
                             src_ap[LASTP * T * k:E * k].rearrange("(p t) -> p t", p=1)).then_inc(s_raw, 16)
            sp.dma_start(nxt[0:LASTP, :], bass.AP(ins["dst"].tensor, T, [[T, LASTP], [1, 2]])).then_inc(s_next, 16)
            sp.wait_ge(s_xfill, 1)
            sp.dma_start(X[:, 0:FULLB, :], rows(ins["x"][0:FULLB * P, :])).then_inc(s_x, 16)
            sp.dma_start(X[0:RESTB, FULLB, :], ins["x"][FULLB * P:N, :]).then_inc(s_x, 16)
            for name in WORDS:
                r, (a, w) = (HID if name == "W2" else C) + 1, WORDS[name]
                for dst_ap, src_ap in ((wts[0:r - 1, a:a + w], ins[name]), (wts[r - 1:r, a:a + w], ins["b" + name])):
                    sp.dma_start(dst_ap, src_ap).then_inc(s_x, 16)
            for name, a in ROWS.items():
                sp.dma_start(bn[:, a:a + C], ins[name].broadcast_to([P, C])).then_inc(s_x, 16)
            for h in range(2):
                sp.wait_ge(s_scat[h], SLOT * HALVES)
            with sp.If(is_unsorted(sp)):
                for k in range(2):
                    for h in range(2):
                        sp.wait_ge(d_scat[h], SLOT * HALVES * (k + 1))
                    if k == 0:
                        sp.dma_start(rec.rearrange("p t f -> p (t f)"),
                                     rec_a.rearrange("(p t) f -> p (t f)", p=P)).then_inc(s_resort, 16)
            with sp.Else():
                sp.wait_ge(s_packed, 1)
                sp.dma_start(rec_b.rearrange("(p t) f -> p (t f)", p=P), rec.rearrange("p t f -> p (t f)")).then_inc(s_copied, 16)
                sp.wait_ge(s_copied, 16)
            sp.wait_ge(s_pfill, 1)
            for k, (sorted_rec, key) in enumerate(((rec_c, SRC), (rec_b, DST))):
                if k:
                    sp.wait_ge(s_ex, BLK.ranges)
                tiles = sorted_rec.rearrange("(j p e) f -> p j e f", p=P, e=P)
                sp.dma_start(recs.rearrange("p j e f -> p j (e f)"), tiles.rearrange("p j e f -> p j (e f)")).then_inc(s_recs, 16)
                last = tiles[:, :, P - 1, 0:2]
                sp.dma_start(c_prev[1:P, :, :], last[0:P - 1, :, :]).then_inc(s_prev, 16)
                sp.dma_start(c_prev[0:1, 1:CHUNKS, :], last[P - 1:P, 0:CHUNKS - 1, :]).then_inc(s_prev, 16)
            sp.wait_ge(s_wfill, 1)
            for n, (kind, k, _) in enumerate(PLAN):
                sp.wait_ge(s_row, n + 1)
                if kind == "B":
                    for j in range(2):
                        sp.dma_start(wbd[K3 * j:K3 * j + K3, :, C * j:C * j + C], ins[f"WS{k + 1}"]).then_inc(s_late, 16)
                sp.dma_start(rows(table), H[:, :, :]).then_inc(s_table, 16)
            sp.wait_ge(s_result, 1)
            sp.dma_start(rows(out[0:FULLB * P, :]), Z[:, 0:FULLB, :]).then_inc(s_out, 16)
            sp.dma_start(out[FULLB * P:N, :], Z[0:RESTB, FULLB, :]).then_inc(s_out, 16)
            sp.wait_ge(s_out, 32)

        @block.gpsimd
        def _(pool):
            def scatter(k, dst_rec, staged, scattered):
                with pool.Fori(0, HALVES) as it:
                    for h in range(2):
                        pool.wait_ge(staged, it * 2 + (2 * HALVES * k + h + 1))
                        pool.sem_inc(s_gate, 1)
                        for u in range(UNIT):
                            pool.indirect_dma_start(
                                out=dst_rec, out_offset=bass.IndirectOffsetOnAxis(ap=posi[:, h, u:u + 1], axis=0),
                                in_=stage[:, h, u * REC:(u + 1) * REC], in_offset=None).then_inc(scattered[h], 16)
            scatter(0, rec_c, s_staged, s_scat)
            with pool.If(is_unsorted(pool)):
                scatter(0, rec_a, d_staged, d_scat)
                scatter(1, rec_b, d_staged, d_scat)
            done = 0
            for n, (kind, k, _) in enumerate(PLAN):
                items = BLK if kind == "A" else SPL
                pool.wait_ge(s_table, 16 * (n + 1))
                pool.sem_inc(s_gate, 1)
                with pool.Fori(0, items.loops) as it:
                    for m in range(SETS):
                        pool.wait_ge(s_idx, it * SETS + (done + m + 1))
                        pool.sem_inc(s_gate, 1)
                        for u in range(UNIT):
                            pool.indirect_dma_start(
                                out=gat[:, m, u, 0:C], out_offset=None, in_=table,
                                in_offset=bass.IndirectOffsetOnAxis(ap=idx[:, m, u:u + 1], axis=0)).then_inc(s_gat[kind][m], 16)
                done += items.units

        @block.scalar
        def _(act):
            sqrt_no = 0

            def sqrts(*pairs):
                nonlocal sqrt_no
                sqrt_no += 1
                act.wait_ge(s_sqin, sqrt_no)
                for dst_ap, src_ap in pairs:
                    last = act.sqrt(dst_ap, src_ap)
                last.then_inc(s_sqout, 1)

            def stage_records(k, pos, staged, scattered):
                def staging(it):
                    for h in range(2):
                        wait(act, scattered[h], it * SLOT + SLOT * HALVES * k)
                        act.wait_ge(pos, it * 2 + (2 * HALVES * k + h + 1))
                        act.copy(posi[:, h, :], posf[:, h, :])
                        act.copy(stage[:, h, :].rearrange("p (u f) -> p u f", f=REC),
                                 rec[:, bass.ds(it * (2 * UNIT) + h * UNIT, UNIT), :]).then_inc(staged, 1)
                turns(act, HALVES, staging, peel=(k == 0))
            stage_records(0, s_pos, s_staged, s_scat)
            with act.If(is_unsorted(act)):
                for h in range(2):
                    act.wait_ge(s_scat[h], SLOT * HALVES)
                stage_records(0, d_pos, d_staged, d_scat)
                act.wait_ge(s_resort, 16)
                stage_records(1, d_pos, d_staged, d_scat)

            for n, (kind, k, tab) in enumerate(PLAN):
                if n in (0, 3, 6, 9):
                    sqrts((st2[:, :], st[:, :]))
                act.wait_ge(s_table, 16 * (n + 1))
                if kind == "A":
                    def stage_a(it):
                        for m in range(SETS):
                            wait(act, a_mm, it * SETS + (k * BLK.units + m + 1 - SETS) if n or not isinstance(it, int) else 0)
                            act.copy(idx[:, m, :], tab[0][:, bass.ds(it * BATCH + m * UNIT, UNIT)]).then_inc(s_idx, 1)
                    turns(act, BLK.loops, stage_a, peel=(n == 0))
                else:
                    ub = k * SPL.units
                    for m in range(SETS):
                        act.copy(idx[:, m, :], spl_row[:, m * UNIT:(m + 1) * UNIT]).then_inc(s_idx, 1)

                    def stage_b(it, more=True):
                        wait(act, b_out, it + k * SPL.loops)
                        for m in range(SETS):
                            act.wait_ge(b_y, it * SETS + (ub + m + 1))
                            for q in range(2):
                                i0 = 16 * (2 * m + q)
                                last = act.copy(ybuf[:, :, i0:i0 + 16].rearrange("p c i -> p i c"),
                                                ps[2 * (m % 2) + q][:, :].rearrange("p (i c) -> p i c", c=C))
                            last.then_inc(b_ev, 1)
                            if more:
                                act.copy(idx[:, m, :], spl_row[:, bass.ds((it + 1) * BATCH + m * UNIT, UNIT)]).then_inc(s_idx, 1)
                    turns(act, SPL.loops - 1, stage_b, peel=(k == 0))
                    stage_b(SPL.loops - 1, more=False)
                    sqrts((bst2[:, :], bst[:, :]))
                if n == 0:
                    sqrts((ndst[:, :], st2[:, :]))
                if n == 3:
                    sqrts((nsrc[:, :], st2[:, :]))

        @block.tensor
        def _(pe):
            asked = 0

            def request(it=0, per=0):
                nonlocal asked
                asked += 1
                pe.wait_ge(s_tope, it * per + asked)

            request()
            pe.matmul(ps[0][0:1, 0:1], ones[:, 0:1], falls[:, 0:1], start=True, stop=True).then_inc(s_frpe, 1)

            def digit_starts(k, nd, tope, frpe, before_it):
                pe.wait_ge(tope, before_it + 1)
                pe.matmul(ps[1][0:nd, 0:1], hist[:, 0:nd], ones[:, 0:1], start=True, stop=True).then_inc(frpe, 1)
                pe.wait_ge(tope, before_it + 2)
                pe.matmul(ps[1][:, P:P + nd], before, hist[:, 0:nd], start=True, stop=False)
                pe.matmul(ps[1][:, P:P + nd], totb[0:nd, :], before[0:nd, 0:nd], start=False, stop=True).then_inc(frpe, 1)
            digit_starts(0, SORTS[0][2], s_tope, s_frpe, asked)
            asked += 2
            with pe.If(is_unsorted(pe)):
                digit_starts(1, SORTS[1][2], d_tope, d_frpe, 0)
                digit_starts(2, SORTS[2][2], d_tope, d_frpe, 2)
            n = 0
            for b, (items, fields) in enumerate(BUILD):
                for r in range(items.ranges):
                    n += 1
                    chunks = items.chunks(r)
                    pe.wait_ge(s_em, n)
                    w = items.width
                    for f, field in enumerate((None,) + fields):
                        for j in chunks:
                            lhs = tileb[:, j, :] if field is None else recs[:, j, :, field]
                            mm = pe.matmul(ps[f][:, 0:w], lhs, emat[:, j, 0:w], start=(j == chunks[0]), stop=(j == chunks[-1]))
                    mm.then_inc(s_ex, 1)

            def linear_chunk(it, name, per, banks, hidden=False):
                t0, t1, result = (ps[b] for b in banks)
                request(it, per)
                for b in range(7):
                    mm = pe.matmul((t0, t1)[b // 4][0:C, (b % 4) * P:(b % 4 + 1) * P], hc[:, b, :], ident, start=True, stop=True)
                mm.then_inc(s_frpe, 1)
                request(it, per)
                if hidden:
                    pe.sem_inc(s_pegate, 1)
                    pe.matmul(t0[0:HID, :], W("W1"), xt[:, 0:512], start=True, stop=True)
                    pe.matmul(t1[0:HID, 0:384], W("W1"), xt[:, 512:896], start=True, stop=True).then_inc(s_frpe, 1)
                    request(it, per)
                for b in range(7):
                    mm = pe.matmul(result[:, b * C:(b + 1) * C], (ht if hidden else xt)[:, b * P:(b + 1) * P], W(name),
                                   start=True, stop=True)
                mm.then_inc(s_frpe, 1)

            def linear(name, hidden=False):
                nonlocal asked
                per, base = (3 if hidden else 2), asked
                with pe.Fori(0, 7) as it:
                    linear_chunk(it, name, per, (0, 1, 2), hidden)
                asked = base + 7 * per

            for n, (kind, k, _) in enumerate(PLAN):
                gb = SLOT * (k * BLK.loops + 1)
                if n == 9:
                    linear("W2", hidden=True)
                if kind == "A":
                    with pe.Fori(0, BLK.loops) as it:
                        for m in range(SETS):
                            pe.wait_ge(s_gat["A"][m], it * SLOT + gb)
                            pe.wait_ge(a_oh, it * SETS + (k * BLK.units + m + 1))
                            for u in range(UNIT):
                                mm = pe.matmul(ps[m][:, u * YW:(u + 1) * YW], mbuf[:, m % 2, u, :], gat[:, m, u, :],
                                               start=True, stop=True)
                            mm.then_inc(a_mm, 1)
                else:
                    ub = k * SPL.units
                    pe.wait_ge(s_late, 32 * (k + 1))

                    def spline(it, root=False):
                        for m in range(SETS):
                            if root and m == 2:
                                linear_chunk(it - 1, f"R{k + 1}", 2, (5, 6, 7))
                            pe.wait_ge(b_prod, it * SETS + (ub + m + 1))
                            if m >= 2 or k or not isinstance(it, int):
                                pe.wait_ge(b_ev, it * SETS + (ub + m - 1))
                            for u in range(UNIT):
                                p0, c0 = K3 * (u % 2), 8 * C * (u // 2 % 2)
                                mm = pe.matmul(ps[2 * (m % 2) + u // 4][p0:p0 + K3, c0:c0 + 8 * C],
                                               bbuf[:, m % 2, u, :], pbuf[:, m % 2, u, :], start=True, stop=True)
                            mm.then_inc(b_y, 1)
                        pe.wait_ge(b_ev, it * SETS + (ub + SETS))
                        for c in range(C):
                            mm = pe.matmul(ps[4][0:2 * C, 0:4 * BATCH], wbd[:, c, :], ybuf[:, c, :], start=(c == 0), stop=(c == C - 1))
                        mm.then_inc(b_out, 1)
                    spline(0)
                    base = asked
                    with pe.Fori(1, 8) as it:
                        spline(it, root=True)
                    asked = base + 14
                    with pe.Fori(8, SPL.loops) as it:
                        spline(it)
                    request()
                    for t in range(NB):
                        mm = pe.matmul(ps[t // 16][:, (t % 16) * C:(t % 16 + 1) * C], aggt[:, t * P:(t + 1) * P], ident2, start=True, stop=True)
                    mm.then_inc(s_frpe, 1)
                    for _ in range(2):
                        request()
                        pe.matmul(ps[0][:, 0:C], ones, bst[:, :], start=True, stop=True).then_inc(s_frpe, 1)
            linear("Wg")

        @block.vector
        def _(dve):
            v = nc.vector
            step = Steps(dve, s_dve)
            to_pe = Steps(dve, s_tope, s_frpe)
            to_act = Steps(dve, s_sqin, s_sqout)

            def per_node(ap):
                return ap.unsqueeze(2).to_broadcast([P, NB, C])

            def per_feature(ap):
                return ap.unsqueeze(1).to_broadcast([P, NB, C])

            step(v.memset(raw_d, PADNODE))
            step(v.memset(raw_s, PADNODE))
            step(v.memset(raw_w, 0.0))
            step(v.memset(nxt[:, :], PADNODE))
            v.memset(raw_a, 0.0).then_inc(s_raw_fill, 1)
            dve.wait_ge(s_raw_fill, 1)
            v.memset(X[:, :, :], 0.0).then_inc(s_xfill, 1)
            v.memset(c_prev[:, :, :], 0.0).then_inc(s_pfill, 1)
            step(v.memset(gat[:, :, :, :], 1.0))
            step(v.memset(rec[:, :, 6:REC], 0.0))
            dve.wait_ge(s_raw, 16 * 8)
            step(v.tensor_copy(rec[:, :, DST], raw_d))
            step(v.tensor_copy(rec[:, :, SRC], raw_s))
            step(v.tensor_copy(rec[:, :, WGT], raw_w))
            step(v.tensor_copy(rec[:, :, ATT:ATT + 3], raw_a.rearrange("p (t f) -> p t f", f=3)))
            v.sem_inc(s_packed, 1)
            dve.wait_ge(s_const, 16)

            step(v.tensor_tensor(eqall[:, 0:T - 1], rec[:, 0:T - 1, DST], rec[:, 1:T, DST], ALU.is_gt))
            step(v.tensor_reduce(falls[:, 0:1], eqall[:, 0:T - 1], AX.X, ALU.add))
            dve.wait_ge(s_next, 16)
            step(v.tensor_tensor(falls[:, 1:2], rec[:, T - 1, DST:DST + 1], nxt[:, 0:1], ALU.is_gt))
            to_pe(v.tensor_tensor(falls[:, 0:1], falls[:, 0:1], falls[:, 1:2], ALU.add))
            v.tensor_copy(flag[:, :], ps[0][0:1, 0:1]).then_inc(s_flagged, 1)

            def sort(number, k, step, to_pe, pos, staged):
                field, shift, nd, more = SORTS[number]
                if more:
                    dve.wait_ge(s_resort, 16)
                step(v.tensor_copy(digit_i, rec[:, :, field]))
                step(v.tensor_scalar(digit_i, digit_i, shift, None, ALU.logical_shift_right))
                if number == 1:
                    step(v.tensor_scalar(digit_i, digit_i, nd - 1, None, ALU.bitwise_and))
                step(v.tensor_copy(digit, digit_i))
                with dve.Fori(0, nd) as d:
                    step.enter(d, 2)
                    step(v.tensor_scalar(eqall, digit, iota[:, bass.ds(d, 1)], None, ALU.is_equal))
                    step(v.tensor_reduce(hist[:, bass.ds(d, 1)], eqall, AX.X, ALU.add))
                    step.leave(nd)
                to_pe(v.memset(tot[:, :], 0.0))
                step(v.tensor_copy(tot[0:nd, :], ps[1][0:nd, 0:1]))
                to_pe(v.tensor_copy(totb[0:nd, :], tot[0:nd, :].to_broadcast([nd, P])))
                step(v.tensor_copy(run[:, 0:nd], ps[1][:, P:P + nd]))

                def positions(it):
                    for h in range(2):
                        wait(dve, staged, it * 2 + (2 * HALVES * k + h - 1) if k or not isinstance(it, int) else 0)
                        for u in range(UNIT):
                            col = it * (2 * UNIT) + (h * UNIT + u)
                            step(v.tensor_scalar(oh[:, 0:nd], iota[:, 0:nd], digit[:, bass.ds(col, 1)], None, ALU.is_equal))
                            step(v.tensor_tensor_reduce(out=oh2[:, 0:nd], in0=oh[:, 0:nd], in1=run[:, 0:nd], scale=1.0, scalar=0.0,
                                                        op0=ALU.mult, op1=ALU.add, accum_out=posf[:, h, u:u + 1]))
                            add = v.tensor_tensor(run[:, 0:nd], run[:, 0:nd], oh[:, 0:nd], ALU.add)
                            if u < UNIT - 1:
                                step(add)
                            else:
                                add.then_inc(pos, 1)
                                dve.wait_ge(pos, it * 2 + (2 * HALVES * k + h + 1))
                peeled = int(k == 0)
                if peeled:
                    positions(0)
                with dve.Fori(peeled, HALVES) as it:
                    step.enter(it, 2 * (3 * UNIT - 1), peeled)
                    positions(it)
                    step.leave(HALVES - peeled)

            sort(0, 0, step, to_pe, s_pos, s_staged)
            with dve.If(is_unsorted(dve)):
                dve.wait_ge(s_staged, 2 * HALVES)
                d_step, d_to_pe = Steps(dve, d_dve), Steps(dve, d_tope, d_frpe)
                sort(1, 0, d_step, d_to_pe, d_pos, d_staged)
                sort(2, 1, d_step, d_to_pe, d_pos, d_staged)

            for j in range(CHUNKS):
                last = v.tensor_copy(tileb[:, j, :], tile_no[:, j:j + 1].to_broadcast([P, P]))
            step(last)
            n = 0
            for b, (items, fields) in enumerate(BUILD):
                if b < 2:
                    dve.wait_ge(s_recs, 16 * (b + 1))
                    dve.wait_ge(s_prev, 32 * (b + 1))
                step(v.tensor_copy(c_i[:, 0, :], recs[:, :, P - 1, fields[0]]))
                step(v.tensor_copy(c_i[:, 1, :], c_prev[:, :, fields[0]]))
                step(v.tensor_scalar(c_i[:, :, :], c_i[:, :, :], items.shift, None, ALU.logical_shift_right))
                step(v.tensor_copy(c_hi[:, :, :], c_i[:, :, :]))
                step(v.tensor_tensor(c_hi[:, 0, :], c_hi[:, 0, :], tile_no, ALU.add))
                step(v.tensor_tensor(c_hi[:, 1, :], c_hi[:, 1, :], tile_no, ALU.add))
                step(v.tensor_scalar(c_hi[:, 1, :], c_hi[:, 1, :], -1.0, None, ALU.add))
                for r in range(items.ranges):
                    w, a = items.width, r * items.width
                    nos = item_no[:, a:a + w]
                    n += 1
                    chunks = items.chunks(r)
                    for j in chunks:
                        step(v.tensor_scalar(emat1[:, 0:w], nos, c_hi[:, 0, j:j + 1], None, ALU.is_le))
                        last = v.scalar_tensor_tensor(emat[:, j, 0:w], nos, c_hi[:, 1, j:j + 1], emat1[:, 0:w], ALU.is_gt, ALU.mult)
                        if j < chunks[-1]:
                            step(last)
                    last.then_inc(s_em, 1)
                    dve.wait_ge(s_em, n)
                    dve.wait_ge(s_ex, n)
                    step(v.tensor_tensor(grp[:, 0:w], nos, ps[0][:, 0:w], ALU.subtract))
                    table_row, loc, wgt, col = (by_src, by_dst, (spl_row, spl_loc, None, scol))[b]
                    part = 32 * (1, 0, 2)[b]
                    step(v.scalar_tensor_tensor(loc[:, a:a + w], grp[:, 0:w], -float(items.size), ps[1][:, 0:w], ALU.mult, ALU.add))
                    step(v.tensor_copy(table_row[:, a:a + w], ps[2][:, 0:w]))
                    step(v.tensor_scalar(col[:, a:a + w], grp[part:part + 1, 0:w], float(YW if items is BLK else SPL.size), None, ALU.mult))
                    if wgt is not None:
                        step(v.tensor_copy(wgt[:, a:a + w], ps[3][:, 0:w]))
                    if items is SPL:
                        for d in range(3):
                            step(v.tensor_scalar(satt[:, a:a + w, d], ps[3 + d][:, 0:w], 3.0, 0.0, ALU.mult, ALU.max))
                            step(v.tensor_scalar(satt[:, a:a + w, d], satt[:, a:a + w, d], 3.0, None, ALU.min))
            step(v.memset(ht, 1.0))
            step(v.memset(xt, 1.0))
            v.memset(wbd, 0.0).then_inc(s_wfill, 1)
            dve.wait_ge(s_wfill, 1)
            dve.wait_ge(s_x, 16 * (2 + 2 * len(WORDS) + len(ROWS)))

            def layernorm_relu():
                step(v.tensor_reduce(st[:, :], X[:, :, :], AX.X, ALU.add))
                step(v.tensor_scalar(st[:, :], st[:, :], -1.0 / C, None, ALU.mult))
                step(v.tensor_tensor(Z[:, :, :], X[:, :, :], per_node(st[:, :]), ALU.add))
                step(v.tensor_tensor(H[:, :, :], Z[:, :, :], Z[:, :, :], ALU.mult))
                step(v.tensor_reduce(st[:, :], H[:, :, :], AX.X, ALU.add))
                to_act(v.tensor_scalar(st[:, :], st[:, :], 1.0 / C, 1e-5, ALU.mult, ALU.add))
                step(v.reciprocal(st2[:, :], st2[:, :]))
                step(v.tensor_tensor(H[:, :, :], Z[:, :, :], per_node(st2[:, :]), ALU.mult))
                return v.tensor_scalar(H[:, :, :], H[:, :, :], 0.0, None, ALU.max)

            def send_rows(n, ins_):
                ins_.then_inc(s_row, 1)
                dve.wait_ge(s_row, n + 1)

            col_regs = [dve.alloc_register(f"column{u}") for u in range(UNIT)]

            def columns(tab, at, most):
                dve.load(col_regs, tab[0:1, bass.ds(at, UNIT)])
                return [dve.snap(r, min_val=0, max_val=most) for r in col_regs]

            def propagate(k, tab):
                _, loc, wgt, col = tab
                weigh_in_matrix = wgt is not None and k > 3
                step(v.memset(Y[:, :, :], 0.0))
                yflat = Y[:, :, :].rearrange("p b c -> p (b c)")

                def onehots(it, m):
                    for u in range(UNIT):
                        i = bass.ds(it * BATCH + (m * UNIT + u), 1)
                        if weigh_in_matrix:
                            last = v.tensor_scalar(mbuf[:, m % 2, u, :], iota, loc[:, i], wgt[:, i], ALU.is_equal, ALU.mult)
                        else:
                            last = v.tensor_scalar(mbuf[:, m % 2, u, :], iota, loc[:, i], None, ALU.is_equal)
                    if wgt is not None and not weigh_in_matrix:
                        dve.wait_ge(s_gat["A"][m], it * SLOT + SLOT * (k * BLK.loops + 1))
                        at = bass.ds(it * BATCH + m * UNIT, UNIT)
                        last = v.tensor_tensor(gat[:, m, :, 0:C], gat[:, m, :, 0:C],
                                               wgt[:, at].unsqueeze(2).to_broadcast([P, UNIT, C]), ALU.mult)
                    last.then_inc(a_oh, 1)

                def turn(it, more=True):
                    for m in range(SETS):
                        if m < SETS - 1:
                            onehots(it, m + 1)
                        elif more:
                            onehots(it + 1, 0)
                        cols = columns(col, it * BATCH + m * UNIT, (NB - 1) * YW)
                        dve.wait_ge(a_mm, it * SETS + (k * BLK.units + m + 1))
                        for u in range(UNIT):
                            dst_ap = yflat[:, bass.ds(cols[u], YW)]
                            step(v.tensor_tensor(dst_ap, dst_ap, ps[m][:, u * YW:(u + 1) * YW], ALU.add))

                onehots(0, 0)
                with dve.Fori(0, BLK.loops - 1) as it:
                    step.enter(it, SETS * UNIT)
                    turn(it)
                    step.leave(BLK.loops - 1)
                turn(BLK.loops - 1, more=False)

            def linear_chunk(it, dst_ap, banks, hidden=False):
                t0, t1, result = (ps[b] for b in banks)
                to_pe(v.tensor_copy(hc[:, :, :], H[:, bass.ds(it * 7, 7), :]))
                step(v.tensor_copy(xt[0:C, 0:512], t0[0:C, :]))
                to_pe(v.tensor_copy(xt[0:C, 512:896], t1[0:C, 0:384]))
                if hidden:
                    step(v.tensor_scalar(ht[0:HID, 0:512], t0[0:HID, :], 0.0, None, ALU.max))
                    to_pe(v.tensor_scalar(ht[0:HID, 512:896], t1[0:HID, 0:384], 0.0, None, ALU.max))
                step(v.tensor_copy(dst_ap[:, bass.ds(it * 7, 7), :], result[:, 0:7 * C].rearrange("p (b c) -> p b c", c=C)))

            def linear(dst_ap, hidden=False):
                with dve.Fori(0, 7) as it:
                    step.enter(it, 2 + hidden)
                    to_pe.enter(it, 2 + hidden)
                    linear_chunk(it, dst_ap, (0, 1, 2), hidden)
                    step.leave(7)
                    to_pe.leave(7)

            def spline(n, k):
                gb, ub = SLOT * (k * SPL.loops + 1), k * SPL.units
                step(v.memset(aggt, 0.0))

                def products(it, m):
                    at = bass.ds(it * BATCH + m * UNIT, UNIT)
                    step(v.tensor_tensor(hat[:, :, :, :], satt[:, at, :].unsqueeze(3).to_broadcast([P, UNIT, 3, 4]),
                                         iota[:, 0:4].unsqueeze(1).unsqueeze(1).to_broadcast([P, UNIT, 3, 4]), ALU.subtract))
                    step(v.scalar_tensor_tensor(hat2[:, :, :, :], hat[:, :, :, :], -1.0, hat[:, :, :, :], ALU.mult, ALU.min))
                    step(v.tensor_scalar(hat[:, :, :, :], hat2[:, :, :, :], 1.0, 0.0, ALU.add, ALU.max))
                    step(v.tensor_tensor(pair[:, :, :, :], hat[:, :, 1, :].unsqueeze(3).to_broadcast([P, UNIT, 4, 4]),
                                         hat[:, :, 0, :].unsqueeze(2).to_broadcast([P, UNIT, 4, 4]), ALU.mult))
                    step(v.tensor_tensor(oh8[:, :, :], iota[:, 0:8].unsqueeze(1).to_broadcast([P, UNIT, 8]),
                                         spl_loc[:, at].unsqueeze(2).to_broadcast([P, UNIT, 8]), ALU.is_equal))
                    if m >= 2 or k or not isinstance(it, int):
                        dve.wait_ge(b_y, it * SETS + (ub + m - 1))
                    step(v.tensor_tensor(bbuf[:, m % 2, :, :].rearrange("p u (a b) -> p u a b", a=4),
                                         hat[:, :, 2, :].unsqueeze(3).to_broadcast([P, UNIT, 4, 16]),
                                         pair[:, :, :, :].rearrange("p u a b -> p u (a b)").unsqueeze(2).to_broadcast([P, UNIT, 4, 16]), ALU.mult))
                    dve.wait_ge(s_gat["B"][m], it * SLOT + gb)
                    v.tensor_tensor(pbuf[:, m % 2, :, :].rearrange("p u (j c) -> p u j c", j=8),
                                    oh8[:, :, :].unsqueeze(3).to_broadcast([P, UNIT, 8, C]),
                                    gat[:, m, :, 0:C].unsqueeze(2).to_broadcast([P, UNIT, 8, C]), ALU.mult).then_inc(b_prod, 1)
                    dve.wait_ge(b_prod, it * SETS + (ub + m + 1))

                def sums(it):
                    dve.wait_ge(b_out, it + (k * SPL.loops + 1))
                    for m in range(SETS):
                        cols = columns(scol, it * BATCH + m * UNIT, NPAD - SPL.size)
                        for u in range(UNIT):
                            p0, i = C * (u % 2), SPL.size * (m * UNIT // 2 + u // 2)
                            dst_ap = aggt[p0:p0 + C, bass.ds(cols[u], SPL.size)]
                            step(v.tensor_tensor(dst_ap, dst_ap, ps[4][p0:p0 + C, i:i + SPL.size], ALU.add),
                                 lag=int(u < UNIT - 1))

                for m in range(SETS):
                    products(0, m)
                for start, stop, root in ((1, 8, True), (8, SPL.loops, False)):
                    with dve.Fori(start, stop) as it:
                        step.enter(it, SETS * 6 + BATCH + 2 * root, start)
                        products(it, 0)
                        products(it, 1)
                        sums(it - 1)
                        if root:
                            to_pe.enter(it, 2, start)
                            linear_chunk(it - 1, F, (5, 6, 7))
                            to_pe.leave(stop - start)
                        products(it, 2)
                        products(it, 3)
                        step.leave(stop - start)
                sums(SPL.loops - 1)

            def mask_padding():
                step(v.tensor_scalar(Z[:, NB - 1, :], Z[:, NB - 1, :], mask, None, ALU.mult))

            def convolve(n, k):
                spline(n, k)
                to_pe(v.memset(tot[:, :], 0.0))
                for t in range(4):
                    b0, nb = 16 * t, min(16, NB - 16 * t)
                    step(v.tensor_tensor(Z[:, b0:b0 + nb, :], ps[t][:, 0:nb * C].rearrange("p (b c) -> p b c", c=C),
                                         inv[:, b0:b0 + nb].unsqueeze(2).to_broadcast([P, nb, C]), ALU.mult))
                step(v.tensor_tensor(Z[:, :, :], Z[:, :, :], F[:, :, :], ALU.add))
                if k < 2:
                    step(v.tensor_scalar(F[:, :, :], Z[:, :, :], 0.01, None, ALU.mult))
                    step(v.tensor_tensor(Z[:, :, :], Z[:, :, :], F[:, :, :], ALU.max))
                step(v.tensor_tensor(Z[:, :, :], Z[:, :, :], H[:, :, :], ALU.add))
                mask_padding()
                to_pe(v.tensor_reduce(bst[:, :], Z[:, :, :].rearrange("p b c -> p c b"), AX.X, ALU.add))
                step(v.tensor_scalar(bst2[:, :], ps[0][:, 0:C], -1.0 / N, None, ALU.mult))
                step(v.tensor_tensor(Z[:, :, :], Z[:, :, :], per_feature(bst2[:, :]), ALU.add))
                mask_padding()
                step(v.tensor_tensor(F[:, :, :], Z[:, :, :], Z[:, :, :], ALU.mult))
                to_pe(v.tensor_reduce(bst[:, :], F[:, :, :].rearrange("p b c -> p c b"), AX.X, ALU.add))
                to_act(v.tensor_scalar(bst[:, :], ps[0][:, 0:C], 1.0 / N, 1e-5, ALU.mult, ALU.add))
                step(v.reciprocal(bst2[:, :], bst2[:, :]))
                step(v.tensor_tensor(bst2[:, :], bst2[:, :], row(f"g{k + 1}"), ALU.mult))
                step(v.tensor_tensor(H[:, :, :], Z[:, :, :], per_feature(bst2[:, :]), ALU.mult))
                return v.tensor_tensor(H[:, :, :], H[:, :, :], per_feature(row(f"be{k + 1}")), ALU.add)

            send_rows(0, layernorm_relu())
            step(v.tensor_scalar(F[:, :, :], H[:, :, :], 0.25, None, ALU.mult))
            for k in range(3):
                propagate(k, by_dst)
                if k == 0:
                    to_act(v.tensor_scalar(st2[:, :], Y[:, :, C], 1.0, 1.0, ALU.add, ALU.max))
                    step(v.tensor_scalar(inv[:, :], Y[:, :, C], 1.0, None, ALU.max))
                    step(v.reciprocal(inv[:, :], inv[:, :]))
                    step(v.reciprocal(ndst[:, :], ndst[:, :]))
                mean = v.tensor_tensor(H[:, :, :], Y[:, :, 0:C], per_node(inv[:, :]), ALU.mult)
                if k < 2:
                    send_rows(k + 1, mean)
                else:
                    step(mean)
                step(v.tensor_scalar(Z[:, :, :], H[:, :, :], 0.25, None, ALU.mult))
                step(v.tensor_tensor(F[:, :, :], F[:, :, :], Z[:, :, :], ALU.add))
            step(v.tensor_tensor(X[:, :, :], X[:, :, :], F[:, :, :], ALU.add))
            send_rows(3, layernorm_relu())
            for k in range(3, 6):
                propagate(k, by_src)
                if k == 3:
                    to_act(v.tensor_scalar(st2[:, :], Y[:, :, C], 1.0, 1.0, ALU.add, ALU.max))
                    step(v.reciprocal(nsrc[:, :], nsrc[:, :]))
                if k < 5:
                    send_rows(k + 1, v.tensor_copy(H[:, :, :], Y[:, :, 0:C]))
            step(v.tensor_tensor(X[:, :, :], X[:, :, :], Y[:, :, 0:C], ALU.add))
            send_rows(6, layernorm_relu())
            for k in range(3):
                last = convolve(6 + k, k)
                if k < 2:
                    send_rows(7 + k, last)
                else:
                    step(last)
            step(v.tensor_tensor(X[:, :, :], X[:, :, :], H[:, :, :], ALU.add))
            step(layernorm_relu())
            linear(F, hidden=True)
            step(v.tensor_scalar(F[:, :, :], F[:, :, :], 0.0, None, ALU.max))
            send_rows(9, v.tensor_tensor(H[:, :, :], F[:, :, :], per_node(nsrc[:, :]), ALU.mult))
            propagate(6, by_dst)
            step(v.tensor_tensor(H[:, :, :], Y[:, :, 0:C], H[:, :, :], ALU.add))
            step(v.tensor_tensor(H[:, :, :], H[:, :, :], per_node(ndst[:, :]), ALU.mult))
            linear(Z)
            step(v.tensor_scalar(Z[:, :, :], Z[:, :, :], 0.0, None, ALU.max))
            step(v.tensor_tensor(Z[:, :, :], Z[:, :, :], F[:, :, :], ALU.add))
            v.tensor_tensor(Z[:, :, :], Z[:, :, :], X[:, :, :], ALU.add).then_inc(s_result, 1)


def kernel(**inputs):
    import numpy as np
    import concourse.bacc as bacc
    from concourse.bass_utils import run_bass_kernel_spmd as run

    nc = bacc.Bacc("TRN2", target_bir_lowering=False, num_devices=1)
    p = np.arange(P)
    consts = np.zeros((P, CW), np.float32)
    for name, value in (("iota", p[None, :]), ("ident", np.eye(P)), ("before", p[:, None] < p[None, :]), ("ones", 1.0),
                        ("tile", np.arange(CHUNKS)[None, :] * P + p[:, None]),
                        ("mask", ((NB - 1) * P + p < N)[:, None]), ("items", np.arange(SPL.n)[None, :]),
                        ("ident2", p[:, None] % C == np.arange(C)[None, :])):
        a, w = CONSTS[name]
        consts[:, a:a + w] = value
    flat = lambda name: np.ascontiguousarray(inputs[name]).reshape(-1)
    mat = lambda name: np.ascontiguousarray(inputs[name])
    vec = lambda name: np.ascontiguousarray(inputs[name]).reshape(1, -1)
    arrays = {"consts": consts, "x": mat("x"), "src": flat("src"), "dst": flat("dst"),
              "edge_weight": flat("edge_weight"), "edge_attr_3": flat("edge_attr_3")}
    for k in (1, 2, 3):
        arrays[f"WS{k}"] = mat(f"L2_gnn_W{k}")
        arrays[f"R{k}"], arrays[f"bR{k}"] = mat(f"L2_gnn_R{k}"), vec(f"L2_gnn_b{k}")
        arrays[f"g{k}"], arrays[f"be{k}"] = vec(f"L2_gnn_g{k}"), vec(f"L2_gnn_be{k}")
    for w, b in (("W1", "b1"), ("W2", "b2"), ("Wg", "bg")):
        arrays[w], arrays["b" + w] = mat("L3_gnn_" + w), vec("L3_gnn_" + b)
    ins = {name: nc.dram_tensor(f"in_{name}", a.shape, mybir.dt.from_np(a.dtype), kind="ExternalInput").ap()
           for name, a in arrays.items()}
    out = nc.dram_tensor("out", (N, C), F32, kind="ExternalOutput").ap()
    build(nc, ins, out)
    r = run(nc, [{f"in_{name}": a for name, a in arrays.items()}], core_ids=[0])
    return r.results[0]["out"]
```
